# Optimizing a Trainium2 kernel written in Bass

```python
import numpy as np
import jax
import jax.numpy as jnp

def _softmax(x, axis=-1):
    return jax.nn.softmax(x, axis=axis)

def _gelu(x):
    return jax.nn.gelu(x, approximate=True)

def _silu(x):
    return jax.nn.silu(x)

def _sigmoid(x):
    return jax.nn.sigmoid(x)

def _layernorm(x, axis=-1, eps=1e-05):
    m = jnp.mean(x, axis=axis, keepdims=True)
    v = jnp.var(x, axis=axis, keepdims=True)
    return (x - m) / jnp.sqrt(v + eps)

def _scatter_add(tgt, idx, src, axis=0):
    return tgt.at[idx].add(src)

def _segment_sum(src, seg, n):
    return jax.ops.segment_sum(src, seg, n)
kernel_name = 'mk_sandwich_d1_jaxref_r8_56838a'

def setup_inputs(seed: int=0):
    np.random.seed(seed)
    _w = jnp.asarray

    def _L0_attn_setup():
        import jax, jax.numpy as jnp
        import numpy as np
        key = jax.random.key(seed)
        k1, k2, k3 = jax.random.split(key, 3)
        N, S, D = (8, 256, 128)
        x = jax.random.normal(k1, (N, S, D), dtype=jnp.float32)
        std = np.sqrt(2.0 / D).astype(np.float32)
        w_lhs = jax.random.normal(k2, (1, 1, D), dtype=jnp.float32) * std
        w_rhs = jax.random.normal(k3, (1, 1, D), dtype=jnp.float32) * std
        return {'x': x, 'w_lhs': w_lhs, 'w_rhs': w_rhs}
    _L0_attn_in = _L0_attn_setup()

    def _L0_ffn_setup():
        import jax, jax.numpy as jnp
        import numpy as np
        D_IN, D_HID = (128, 512)

        def _ternary(key, shape):
            return jax.random.randint(key, shape, -1, 2).astype(jnp.float32)

        def _tlin(x, w, s):
            return jnp.einsum('bsi,oi->bso', x, w) * s
        key = jax.random.key(seed)
        ks = jax.random.split(key, 12)
        inv = lambda fan: 1.0 / np.sqrt(fan).astype(np.float32)
        return {'x': jax.random.normal(ks[0], (4, 256, D_IN), dtype=jnp.float32), 'w1_w': _ternary(ks[1], (D_HID, D_IN)), 'w1_s': jax.random.uniform(ks[2], (D_HID,), dtype=jnp.float32) * inv(D_IN), 'w2_w': _ternary(ks[3], (D_HID, D_IN)), 'w2_s': jax.random.uniform(ks[4], (D_HID,), dtype=jnp.float32) * inv(D_IN), 'h1_w': _ternary(ks[5], (D_HID, D_HID)), 'h1_s': jax.random.uniform(ks[6], (D_HID,), dtype=jnp.float32) * inv(D_HID), 'h2_w': _ternary(ks[7], (D_HID, D_HID)), 'h2_s': jax.random.uniform(ks[8], (D_HID,), dtype=jnp.float32) * inv(D_HID), 'w3_w': _ternary(ks[9], (D_IN, D_HID)), 'w3_s': jax.random.uniform(ks[10], (D_IN,), dtype=jnp.float32) * inv(D_HID)}
    _L0_ffn_in = _L0_ffn_setup()
    _d = {'L0_attn_x': _L0_attn_in['x'], 'L0_attn_w_lhs': _L0_attn_in['w_lhs'], 'L0_attn_w_rhs': _L0_attn_in['w_rhs'], 'L0_ffn_w1_w': _L0_ffn_in['w1_w'], 'L0_ffn_w1_s': _L0_ffn_in['w1_s'], 'L0_ffn_w2_w': _L0_ffn_in['w2_w'], 'L0_ffn_w2_s': _L0_ffn_in['w2_s'], 'L0_ffn_h1_w': _L0_ffn_in['h1_w'], 'L0_ffn_h1_s': _L0_ffn_in['h1_s'], 'L0_ffn_h2_w': _L0_ffn_in['h2_w'], 'L0_ffn_h2_s': _L0_ffn_in['h2_s'], 'L0_ffn_w3_w': _L0_ffn_in['w3_w'], 'L0_ffn_w3_s': _L0_ffn_in['w3_s']}
    _x0 = _d['L0_attn_x']
    _d['L0_attn_x'] = jax.random.normal(jax.random.fold_in(jax.random.key(seed), 1), (16, 512, 128), dtype=_x0.dtype)
    del _x0
    return _d

def reference(L0_attn_x, L0_attn_w_lhs, L0_attn_w_rhs, L0_ffn_w1_w, L0_ffn_w1_s, L0_ffn_w2_w, L0_ffn_w2_s, L0_ffn_h1_w, L0_ffn_h1_s, L0_ffn_h2_w, L0_ffn_h2_s, L0_ffn_w3_w, L0_ffn_w3_s):

    def _L0_attn_ref(x, w_lhs, w_rhs):
        import jax, jax.numpy as jnp
        import numpy as np
        lhs = x * w_lhs
        rhs = x * w_rhs
        scores = jnp.einsum('nsd,ntd->nst', lhs, rhs)
        attn = jax.nn.softmax(scores, axis=2)
        return jnp.einsum('nst,ntd->nsd', attn, x)

    def _L0_ffn_ref(x, w1_w, w1_s, w2_w, w2_s, h1_w, h1_s, h2_w, h2_s, w3_w, w3_s):
        import jax, jax.numpy as jnp
        import numpy as np
        D_IN, D_HID = (128, 512)

        def _ternary(key, shape):
            return jax.random.randint(key, shape, -1, 2).astype(jnp.float32)

        def _tlin(x, w, s):
            return jnp.einsum('bsi,oi->bso', x, w) * s
        h = jax.nn.silu(_tlin(x, w1_w, w1_s)) * _tlin(x, w2_w, w2_s)
        h = jax.nn.gelu(_tlin(h, h1_w, h1_s), approximate=False)
        h = jax.nn.gelu(_tlin(h, h2_w, h2_s), approximate=False)
        return _tlin(h, w3_w, w3_s)
    x = L0_attn_x
    x = x + _layernorm(_L0_attn_ref(_layernorm(x, axis=-1), L0_attn_w_lhs, L0_attn_w_rhs), axis=-1)
    x = x + _layernorm(_L0_ffn_ref(_layernorm(x, axis=-1), L0_ffn_w1_w, L0_ffn_w1_s, L0_ffn_w2_w, L0_ffn_w2_s, L0_ffn_h1_w, L0_ffn_h1_s, L0_ffn_h2_w, L0_ffn_h2_s, L0_ffn_w3_w, L0_ffn_w3_s), axis=-1)
    return x

_drawn_inputs = setup_inputs


def setup_inputs(seed=0):
    import zlib

    import numpy as np

    out = dict(_drawn_inputs(seed))
    spreads = {}
    factors = {}
    for name, (base, spread) in spreads.items():
        noise = np.random.default_rng([zlib.crc32(name.encode()), seed]).standard_normal(out[name].shape)
        drawn = base * np.exp(spread * noise) if base else spread * noise
        out[name] = jnp.asarray(drawn.astype(out[name].dtype))
    for name, factor in factors.items():
        out[name] = (out[name] * factor).astype(out[name].dtype)
    return out
```

```python
from contextlib import ExitStack

import concourse.bass as bass
from concourse import mybir


def sandwich_kernel(
    nc: bass.Bass,
    x_dram: bass.AP,
    weights_dram: bass.AP,
    columns_dram: bass.AP,
    out_dram: bass.AP,
):
    f32, f32r, f16, i32 = mybir.dt.float32, mybir.dt.float32r, mybir.dt.float16, mybir.dt.int32
    ALU = mybir.AluOpType
    ACT = mybir.ActivationFunctionType
    AX = mybir.AxisListType

    N, S, D = x_dram.shape
    P = 128
    T = S // P
    K = (columns_dram.shape[1] - 3) // 4
    H = K * P
    W = weights_dram.shape[1]
    EPS = 1e-5
    W1, W2, W3 = 0, H, 2 * H
    H1, H2 = 3 * H, 3 * H + K * H
    S1, S2, SH1, SH2, S3, WL, WR = 0, K, 2 * K, 3 * K, 4 * K, 4 * K + 1, 4 * K + 2

    with ExitStack() as ctx:
        def sb(name, shape, dt):
            return ctx.enter_context(nc.sbuf_tensor(name, shape, dt))

        def ps(name):
            return ctx.enter_context(nc.psum_tensor(name, [P, S], f32))

        def sem(name):
            return ctx.enter_context(nc.semaphore(name))

        ident = sb("ident", [P, P], f32)
        ones = sb("ones", [P, P], f32)
        minus_half = sb("minus_half", [P, T], f32)
        columns = sb("columns", [P, 4 * K + 3], f32)
        neg_wlr = sb("neg_wlr", [P, 1], f32)
        w_raw = sb("w_raw", [P, W], f32)
        w_hi = sb("w_hi", [P, W], f32r)
        w_lo = sb("w_lo", [P, W], f32r)
        lo_count = sb("lo_count", [P, 2], f32)
        lo_total = sb("lo_total", [P, 2], f32)
        x_in = sb("x_in", [P, T, D], f32)
        x_res = sb("x_res", [P, T, D], f32)
        xn = sb("xn", [P, T, D], f32)
        xn_hi = sb("xn_hi", [P, T, D], f16)
        xn_lo = sb("xn_lo", [P, T, D], f16)
        x1 = sb("x1", [P, T, D], f32)
        x1_all = sb("x1_all", [P, N, T * D], f32)
        x1_tail = sb("x1_tail", [P, T, D], f32)
        x2n = sb("x2n", [P, T, D], f32)
        att_base = sb("att_base", [P, T, D], f32)
        ffn_base = sb("ffn_base", [P, T, D], f32)
        y_out = sb("y_out", [P, T, D], f32)
        xT_hi = sb("xT_hi", [P, S], f32r)
        xT_lo = sb("xT_lo", [P, S], f32r)
        aT_hi = sb("aT_hi", [P, S], f32r)
        aT_lo = sb("aT_lo", [P, S], f32r)
        x2T_hi = sb("x2T_hi", [P, S], f32r)
        x2T_lo = sb("x2T_lo", [P, S], f32r)
        yT = sb("yT", [P, S], f32)
        neg_max = sb("neg_max", [P, T], f32)
        row_sum = sb("row_sum", [P, T], f32)
        exps = sb("exps", [P, T, S], f32)
        eT_hi = sb("eT_hi", [P, 2, T, P], f16)
        eT_lo = sb("eT_lo", [P, 2, T, P], f16)
        gate = sb("gate", [P, 2, S], f32)
        h_full = sb("h_full", [P, K, S], f32)
        hA_hi, hB_hi = (sb(f"h{c}_hi", [P, K, S], f32r) for c in "AB")
        hA_lo, hB_lo = (sb(f"h{c}_lo", [P, K, S], f32r) for c in "AB")
        hC_hi, hC_lo = hA_hi, hA_lo

        hid_bank = [ps(f"hid_bank{m}") for m in range(4)]
        score_bank = [ps(f"score_bank{m}") for m in range(2)]
        eT_bank = ps("eT_bank")
        mix_bank = ps("mix_bank")
        w3_bank = x2T_bank = eT_bank
        xT_bank = score_bank[0]
        y_bank = mix_bank

        x_loaded = sem("x_loaded")
        x_res_loaded = sem("x_res_loaded")
        w_loaded = sem("w_loaded")
        columns_loaded = sem("columns_loaded")
        out_stored = sem("out_stored")
        x1_saved, x1_tail_loaded = sem("x1_saved"), sem("x1_tail_loaded")
        consts_zeroed = sem("consts_zeroed")
        consts_ready = sem("consts_ready")
        w_hi_ready, w_lo_ready = sem("w_hi_ready"), sem("w_lo_ready")
        lo_counted, lo_summed, lo_known = sem("lo_counted"), sem("lo_summed"), sem("lo_known")
        neg_wlr_ready = sem("neg_wlr_ready")
        xT_turned, x2T_turned, y_turned = sem("xT_turned"), sem("x2T_turned"), sem("y_turned")
        scores_done, eT_turned, pv_done = sem("scores_done"), sem("eT_turned"), sem("pv_done")
        gated_mm, h1_mm, h2_mm = sem("gated_mm"), sem("h1_mm"), sem("h2_mm")
        w3_mm = sem("w3_mm")
        xT_hi_ready = sem("xT_hi_ready")
        exp_done, eT_hi_ready = sem("exp_done"), sem("eT_hi_ready")
        gate_ready, gelu1_done, gelu2_done = sem("gate_ready"), sem("gelu1_done"), sem("gelu2_done")
        yT_ready, x2T_hi_ready = sem("yT_ready"), sem("x2T_hi_ready")
        max_ready, eT_lo_ready = sem("max_ready"), sem("eT_lo_ready")
        gated_done = sem("gated_done")
        hA_lo_ready, hB_lo_ready, hC_lo_ready = (sem(f"h{c}_lo_ready") for c in "ABC")
        xT_lo_ready = sem("xT_lo_ready")
        x2T_lo_ready, xn_lo_ready = sem("x2T_lo_ready"), sem("xn_lo_ready")
        x1_ready, y_ready = sem("x1_ready"), sem("y_ready")
        hA_hi_ready = sem("hA_hi_ready")
        xn_ready, xn_hi_ready, x2n_ready = sem("xn_ready"), sem("xn_hi_ready"), sem("x2n_ready")
        att_base_ready, ffn_base_ready = sem("att_base_ready"), sem("ffn_base_ready")
        rs_chain = sem("rs_chain")

        waits_apart = sem("waits_apart")

        class Norm:
            def __init__(self, name):
                self.stats = sb(f"{name}_stats", [P, T, 6], f32)
                self.mean_var = sb(f"{name}_mean_var", [P, T, 2], f32)
                self.var_eps = sb(f"{name}_var_eps", [P, T], f32)
                self.rstd = sb(f"{name}_rstd", [P, T], f32)
                self.scaled_mean = sb(f"{name}_scaled_mean", [P, T], f32)
                self.shift = sb(f"{name}_shift", [P, T], f32)
                self.stats_done = sem(f"{name}_stats_done")
                self.mean_var_done = sem(f"{name}_mean_var_done")
                self.chain = sem(f"{name}_chain")

        ln_x, ln_att, ln_x1, ln_y = Norm("ln_x"), Norm("ln_att"), Norm("ln_x1"), Norm("ln_y")
        rs_squared = sb("rs_squared", [P, T], f32)
        rs_eps = sb("rs_eps", [P, T], f32)

        def wait(eng, semaphore, per, b, count, apart=False):
            if isinstance(b, int):
                if per * b + count > 0:
                    eng.wait_ge(semaphore, min(per * b + count, per * N))
                return
            eng.wait_ge(semaphore, b * per + count)
            if apart:
                eng.sem_inc(waits_apart, 1)

        def x_view(dram, b):
            return dram[b, :, :].rearrange("(p t) d -> p t d", t=T)

        block = ctx.enter_context(nc.Block())

        class Stages:
            def __init__(self, i, full=False):
                def batch(b):
                    return b if full or 0 <= b < N else None
                self.prep, self.att, self.mid, self.ffn, self.tail = (batch(i + d) for d in (1, 0, -1, -2, -3))

        def steps(eng, step, first=2):
            for i in range(first, 4):
                step(Stages(i))
            with eng.Fori(4, N - 1) as i:
                step(Stages(i, full=True))
            for i in range(N - 1, N + 3):
                step(Stages(i))

        @block.sync
        def _(sp):
            def load_x(b):
                wait(sp, xn_ready, 1, b, 0)
                sp.dma_start(x_in[:, :, :], x_view(x_dram, b)).then_inc(x_loaded, 16)

            def step(st):
                if st.prep is not None:
                    load_x(st.prep)
                if st.att is not None:
                    wait(sp, att_base_ready, 1, st.att, 0)
                    sp.dma_start(x_res[:, :, :], x_view(x_dram, st.att)).then_inc(x_res_loaded, 16)
                if st.mid is not None:
                    wait(sp, x1_ready, 1, st.mid, 1)
                    sp.dma_start(x1_all[:, st.mid, :], x1[:, :, :].rearrange("p t d -> p (t d)")).then_inc(x1_saved, 16)
                if st.tail is not None:
                    g = st.tail
                    wait(sp, x1_saved, 16, g, 16)
                    wait(sp, ffn_base_ready, 1, g, 0)
                    sp.dma_start(x1_tail[:, :, :].rearrange("p t d -> p (t d)"), x1_all[:, g, :]).then_inc(x1_tail_loaded, 16)
                    wait(sp, y_ready, 1, g, 1)
                    sp.dma_start(x_view(out_dram, g), y_out[:, :, :]).then_inc(out_stored, 16)

            load_x(0)
            sp.dma_start(columns[:, :], columns_dram).then_inc(columns_loaded, 16)
            sp.dma_start(w_raw[:, :], weights_dram).then_inc(w_loaded, 16)
            steps(sp, step, first=0)
            sp.wait_ge(out_stored, 16 * N)

        @block.tensor
        def _(pe):
            def matmuls(out, pairs):
                for n, (lhs, rhs) in enumerate(pairs):
                    mm = nc.tensor.matmul(out, lhs, rhs, start=(n == 0), stop=(n == len(pairs) - 1))
                return mm

            def turn(bank, src, done):
                for t in range(T):
                    mm = nc.tensor.transpose(bank[:, t * P:(t + 1) * P], src[:, t * P:(t + 1) * P], ident[:, :])
                mm.then_inc(done, 1)

            def turn_x(b):
                wait(pe, xn_ready, 1, b, 1)
                wait(pe, exp_done, T, b, -1)
                turn(xT_bank, xn[:, :, :].rearrange("p t d -> p (t d)"), xT_turned)

            def scores(b, j):
                if j == 0:
                    wait(pe, xT_lo_ready, 2, b, 2)
                wait(pe, exp_done, T, b, j - 1)
                rows = slice(j * P, (j + 1) * P)
                matmuls(score_bank[j % 2][:, :], [
                    (aT_hi[:, rows], xT_hi[:, :]), (aT_hi[:, rows], xT_lo[:, :]), (aT_lo[:, rows], xT_hi[:, :]),
                ]).then_inc(scores_done, 1)

            def turn_e(b, j):
                wait(pe, exp_done, T, b, j + 1)
                if j == 0:
                    wait(pe, x2T_lo_ready, 1, b, 0)
                wait(pe, eT_lo_ready, T, b, j)
                turn(eT_bank, exps[:, j, :], eT_turned)

            def pv(b, j):
                if j == 0:
                    wait(pe, xn_lo_ready, 1, b, 1)
                    wait(pe, y_ready, 1, b, -2)
                    wait(pe, x1_ready, 1, b, 0)
                wait(pe, eT_lo_ready, T, b, j + 1)
                pairs = []
                for t in range(T):
                    hi, lo = eT_hi[:, j % 2, t, :], eT_lo[:, j % 2, t, :]
                    pairs += [(hi, xn_hi[:, t, :]), (hi, xn_lo[:, t, :]), (lo, xn_hi[:, t, :])]
                matmuls(mix_bank[:, j * P:(j + 1) * P], pairs).then_inc(pv_done, 1)

            def turn_x2(b):
                wait(pe, x2n_ready, 1, b, 1)
                wait(pe, yT_ready, 1, b, -1)
                turn(x2T_bank, x2n[:, :, :].rearrange("p t d -> p (t d)"), x2T_turned)

            def products(general, col, hi, lo):
                w = slice(col, col + P)
                pairs = [(w_hi[:, w], hi), (w_hi[:, w], lo)]
                return pairs + ([(w_lo[:, w], hi)] if general else [])

            def gated(general, b, m):
                if m == 0:
                    wait(pe, x2T_lo_ready, 1, b, 1)
                if m < 2:
                    wait(pe, gelu2_done, K, b, 2 * m + 2 - K)
                else:
                    wait(pe, gated_done, K, b, m - 1)
                for bank, w in ((hid_bank[2 * (m % 2)], W1), (hid_bank[2 * (m % 2) + 1], W2)):
                    mm = matmuls(bank[:, :], products(general, w + m * P, x2T_hi[:, :], x2T_lo[:, :]))
                mm.then_inc(gated_mm, 1)

            def hidden(general, b, tiles, ks, w, hi, lo, lo_ready, bank_read, done):
                for m in tiles:
                    if 0 in ks:
                        bank_read(m)
                    for k in ks:
                        if m == 0:
                            wait(pe, lo_ready, K, b, k + 1)
                        pairs = products(general, w + k * H + m * P, hi[:, k, :], lo[:, k, :])
                        for n, (lhs, rhs) in enumerate(pairs):
                            mm = nc.tensor.matmul(hid_bank[m][:, :], lhs, rhs, start=(k == 0 and n == 0),
                                                  stop=(k == K - 1 and n == len(pairs) - 1))
                    if K - 1 in ks:
                        mm.then_inc(done, 1)

            def layer1(general, b, tiles, ks):
                hidden(general, b, tiles, ks, H1, hA_hi, hA_lo, hA_lo_ready,
                       lambda m: wait(pe, gated_done, K, b, 3 + m // 2), h1_mm)

            def layer2(general, b, tiles, ks):
                hidden(general, b, tiles, ks, H2, hB_hi, hB_lo, hB_lo_ready,
                       lambda m: wait(pe, gelu1_done, K, b, m + 1), h2_mm)

            def layer3(general, b, ks):
                if 0 in ks:
                    wait(pe, eT_lo_ready, T, b, 3 * T)
                for k in ks:
                    wait(pe, hC_lo_ready, K, b, k + 1)
                    pairs = products(general, W3 + k * P, hC_hi[:, k, :], hC_lo[:, k, :])
                    for n, (lhs, rhs) in enumerate(pairs):
                        mm = nc.tensor.matmul(w3_bank[:, :], lhs, rhs, start=(k == 0 and n == 0),
                                              stop=(k == K - 1 and n == len(pairs) - 1))
                if K - 1 in ks:
                    mm.then_inc(w3_mm, 1)

            def turn_y(b):
                wait(pe, yT_ready, 1, b, 1)
                wait(pe, x1_ready, 1, b, 3)
                turn(y_bank, yT, y_turned)

            def make_step(general):
                def step(st):
                    a, f, g = st.att, st.ffn, st.tail
                    if f is not None:
                        gated(general, f, 0)
                    if g is not None:
                        layer3(general, g, (0, 1))
                    if f is not None:
                        gated(general, f, 1)
                    if g is not None:
                        layer3(general, g, (2, 3))
                    if a is not None:
                        scores(a, 0)
                        scores(a, 1)
                    if f is not None:
                        gated(general, f, 2)
                        gated(general, f, 3)
                    if g is not None:
                        turn_y(g)
                    if f is not None:
                        layer1(general, f, (0, 1), (0, 1))
                        layer1(general, f, (0, 1), (2,))
                    if st.mid is not None:
                        turn_x2(st.mid)
                    if a is not None:
                        scores(a, 2)
                        scores(a, 3)
                    if f is not None:
                        layer1(general, f, (0, 1), (3,))
                    if a is not None:
                        turn_e(a, 0)
                    if f is not None:
                        layer1(general, f, (2,), range(K))
                    if a is not None:
                        turn_e(a, 1)
                    if f is not None:
                        layer1(general, f, (3,), range(K))
                    if a is not None:
                        pv(a, 0)
                    if f is not None:
                        layer2(general, f, (0, 1), (0, 1))
                    if a is not None:
                        turn_e(a, 2)
                        pv(a, 1)
                    if f is not None:
                        layer2(general, f, (0, 1), (2,))
                        layer2(general, f, (0, 1), (3,))
                    if a is not None:
                        turn_e(a, 3)
                        pv(a, 2)
                    if st.prep is not None:
                        turn_x(st.prep)
                    if f is not None:
                        layer2(general, f, (2,), range(K))
                    if a is not None:
                        pv(a, 3)
                    if f is not None:
                        layer2(general, f, (3,), range(K))
                return step

            pe.wait_ge(consts_ready, 2)
            turn_x(0)
            common = make_step(False)
            common(Stages(0))
            pe.wait_ge(lo_counted, 2)
            pe.wait_ge(eT_lo_ready, T)
            nc.tensor.matmul(eT_bank[:, 0:2], ones[:, :], lo_count[:, :], start=True, stop=True).then_inc(lo_summed, 1)
            pe.wait_ge(lo_known, 1)
            any_lo = pe.value_load(lo_total[0:1, 0:1].bitcast(i32))
            common(Stages(1))
            with pe.If(any_lo != 0):
                steps(pe, make_step(True))
            with pe.Else():
                steps(pe, make_step(False))

        @block.scalar
        def _(act):
            def split_x(b):
                wait(act, xT_turned, 1, b, 1)
                wait(act, scores_done, T, b, 0)
                nc.scalar.copy(xT_hi[:, :], xT_bank[:, :]).then_inc(xT_hi_ready, 1)
                nc.scalar.mul(aT_hi[:, :], xT_bank[:, :], neg_wlr[:, 0:1]).then_inc(xT_hi_ready, 1)

            def softmax(b, j):
                wait(act, max_ready, T, b, j + 1)
                wait(act, eT_turned, T, b, j + 1 - T)
                nc.scalar.activation(exps[:, j, :], score_bank[j % 2][:, :], ACT.Exp, bias=neg_max[:, j:j + 1],
                                     scale=-1.0, accum_out=row_sum[:, j:j + 1]).then_inc(exp_done, 1)

            def split_e(b, j):
                wait(act, eT_turned, T, b, j + 1)
                wait(act, pv_done, T, b, j - 1)
                nc.scalar.copy(eT_hi[:, j % 2, :, :].rearrange("p t s -> p (t s)"), eT_bank[:, :]).then_inc(eT_hi_ready, 1)

            def silu(b, m):
                wait(act, gated_mm, K, b, m + 1)
                wait(act, gated_done, K, b, m - 1)
                nc.scalar.activation(gate[:, m % 2, :], hid_bank[2 * (m % 2)][:, :], ACT.Silu,
                                     scale=columns[:, S1 + m:S1 + m + 1]).then_inc(gate_ready, 1)

            def gelu(b, m, mm, col, last_lo, hi, hi_used, per, count, done):
                wait(act, mm, K, b, m + 1)
                wait(act, last_lo, K, b, m + 1)
                if m == 0:
                    wait(act, hi_used, per, b, count)
                scale = columns[:, col + m:col + m + 1]
                nc.scalar.activation(h_full[:, m, :], hid_bank[m][:, :], ACT.Gelu, scale=scale)
                nc.scalar.activation(hi[:, m, :], hid_bank[m][:, :], ACT.Gelu, scale=scale).then_inc(done, 1)

            def gelu1(b, m):
                gelu(b, m, h1_mm, SH1, hA_lo_ready, hB_hi, h2_mm, K, 0, gelu1_done)

            def gelu2(b, m):
                gelu(b, m, h2_mm, SH2, hB_lo_ready, hC_hi, h1_mm, K, K, gelu2_done)

            def step(st):
                a, f, g = st.att, st.ffn, st.tail
                if f is not None:
                    silu(f, 0)
                    silu(f, 1)
                if g is not None:
                    wait(act, w3_mm, 1, g, 1)
                    wait(act, y_turned, 1, g, 0)
                    nc.scalar.mul(yT[:, :], w3_bank[:, :], columns[:, S3:S3 + 1]).then_inc(yT_ready, 1)
                if f is not None:
                    silu(f, 2)
                    silu(f, 3)
                if a is not None:
                    softmax(a, 0)
                    softmax(a, 1)
                if st.mid is not None:
                    wait(act, x2T_turned, 1, st.mid, 1)
                    wait(act, gated_mm, K, st.mid, 0)
                    nc.scalar.copy(x2T_hi[:, :], x2T_bank[:, :]).then_inc(x2T_hi_ready, 1)
                if a is not None:
                    softmax(a, 2)
                    softmax(a, 3)
                    split_e(a, 0)
                if f is not None:
                    gelu1(f, 0)
                    gelu1(f, 1)
                if a is not None:
                    split_e(a, 1)
                if f is not None:
                    gelu1(f, 2)
                    gelu1(f, 3)
                if a is not None:
                    split_e(a, 2)
                if f is not None:
                    gelu2(f, 0)
                    gelu2(f, 1)
                if a is not None:
                    split_e(a, 3)
                if st.prep is not None:
                    split_x(st.prep)
                if f is not None:
                    gelu2(f, 2)
                    gelu2(f, 3)

            act.wait_ge(columns_loaded, 16)
            act.wait_ge(neg_wlr_ready, 1)
            split_x(0)
            step(Stages(0))
            act.wait_ge(w_loaded, 16)
            nc.scalar.copy(w_hi[:, :], w_raw[:, :]).then_inc(w_hi_ready, 1)
            steps(act, step, first=1)

        def statistics(norm, b, tile):
            for t in range(T):
                op = nc.vector.bn_stats(norm.stats[:, t, :], tile(t))
            op.then_inc(norm.stats_done, 1)
            wait(nc.vector, norm.stats_done, 1, b, 1, apart=True)
            for t in range(T):
                op = nc.vector.bn_aggr(norm.mean_var[:, t, :], norm.stats[:, t, :])
            op.then_inc(norm.mean_var_done, 1)

        @block.vector
        def _(dve):
            def minus(out, a, b):
                return nc.vector.tensor_tensor(out, a, b, ALU.subtract)

            def row_max(b, j):
                wait(dve, scores_done, T, b, j + 1)
                nc.vector.tensor_reduce(neg_max[:, j:j + 1], score_bank[j % 2][:, :], AX.X, ALU.min).then_inc(max_ready, 1)

            def split_e(b, j):
                wait(dve, eT_hi_ready, T, b, j + 1)
                minus(eT_lo[:, j % 2, :, :].rearrange("p t s -> p (t s)"), eT_bank[:, :],
                      eT_hi[:, j % 2, :, :].rearrange("p t s -> p (t s)")).then_inc(eT_lo_ready, 1)

            def gated(b, m):
                wait(dve, hC_lo_ready, K, b, m + 1 - K)
                wait(dve, gate_ready, K, b, m + 1)
                nc.vector.scalar_tensor_tensor(h_full[:, m, :], hid_bank[2 * (m % 2) + 1][:, :],
                                               columns[:, S2 + m:S2 + m + 1], gate[:, m % 2, :],
                                               ALU.mult, ALU.mult).then_inc(gated_done, 1)

            def high_A(b, m):
                if m == 0:
                    wait(dve, w3_mm, 1, b, 0)
                wait(dve, gated_done, K, b, m + 1)
                nc.vector.tensor_copy(hA_hi[:, m, :], h_full[:, m, :]).then_inc(hA_hi_ready, 1)

            def split_h(b, m, hi_ready, hi, lo, lo_ready):
                wait(dve, hi_ready, K, b, m + 1)
                minus(lo[:, m, :], h_full[:, m, :], hi[:, m, :].bitcast(f32)).then_inc(lo_ready, 1)

            def split_A(b, m):
                split_h(b, m, hA_hi_ready, hA_hi, hA_lo, hA_lo_ready)

            def split_B(b, m):
                split_h(b, m, gelu1_done, hB_hi, hB_lo, hB_lo_ready)

            def split_C(b, m):
                split_h(b, m, gelu2_done, hC_hi, hC_lo, hC_lo_ready)

            def x_statistics(b):
                dve.wait_ge(x_loaded, b * 16 + 16)
                statistics(ln_x, b, lambda t: x_in[:, t, :])

            def split_xn(b):
                wait(dve, xn_hi_ready, 1, b, 1)
                minus(xn_lo[:, :, :], xn[:, :, :], xn_hi[:, :, :]).then_inc(xn_lo_ready, 1)

            def split_x(b):
                wait(dve, xT_hi_ready, 2, b, 2)
                minus(xT_lo[:, :], xT_bank[:, :], xT_hi[:, :].bitcast(f32)).then_inc(xT_lo_ready, 1)
                nc.vector.scalar_tensor_tensor(aT_lo[:, :], xT_bank[:, :], neg_wlr[:, 0:1], aT_hi[:, :].bitcast(f32),
                                               ALU.mult, ALU.subtract).then_inc(xT_lo_ready, 1)

            def scaled_add(norm, b, src, base, base_ready, out, done):
                wait(dve, base_ready, 1, b, 1)
                for t in range(T):
                    op = nc.vector.scalar_tensor_tensor(out[:, t, :], src[:, t * P:(t + 1) * P], norm.rstd[:, t:t + 1],
                                                        base[:, t, :], ALU.mult, ALU.add)
                op.then_inc(done, 1)

            def step(st):
                a, b, f, g = st.att, st.mid, st.ffn, st.tail
                if b is not None:
                    wait(dve, x1_saved, 16, b, 0)
                    wait(dve, x2n_ready, 1, b, 0)
                    scaled_add(ln_att, b, mix_bank, att_base, att_base_ready, x1, x1_ready)
                    wait(dve, x1_ready, 1, b, 1)
                    statistics(ln_x1, b, lambda t: x1[:, t, :])
                if f is not None:
                    gated(f, 0)
                    gated(f, 1)
                    high_A(f, 0)
                if a is not None:
                    row_max(a, 0)
                if f is not None:
                    split_A(f, 0)
                    high_A(f, 1)
                if a is not None:
                    row_max(a, 1)
                if f is not None:
                    split_A(f, 1)
                    gated(f, 2)
                    gated(f, 3)
                    high_A(f, 2)
                    high_A(f, 3)
                    split_A(f, 2)
                    split_A(f, 3)
                if g is not None:
                    wait(dve, y_turned, 1, g, 1)
                    statistics(ln_y, g, lambda t: y_bank[:, t * P:(t + 1) * P])
                if b is not None:
                    wait(dve, x2T_hi_ready, 1, b, 1)
                    minus(x2T_lo[:, :], x2T_bank[:, :], x2T_hi[:, :].bitcast(f32)).then_inc(x2T_lo_ready, 1)
                if a is not None:
                    row_max(a, 2)
                    row_max(a, 3)
                    split_xn(a)
                if g is not None:
                    wait(dve, out_stored, 16, g, 0)
                    scaled_add(ln_y, g, y_bank, ffn_base, ffn_base_ready, y_out, y_ready)
                if a is not None:
                    split_e(a, 0)
                if st.prep is not None:
                    x_statistics(st.prep)
                if f is not None:
                    split_B(f, 0)
                    split_B(f, 1)
                if a is not None:
                    split_e(a, 1)
                if f is not None:
                    split_B(f, 2)
                    split_B(f, 3)
                if a is not None:
                    split_e(a, 2)
                if f is not None:
                    split_C(f, 0)
                    split_C(f, 1)
                if a is not None:
                    split_e(a, 3)
                if st.prep is not None:
                    split_x(st.prep)
                if a is not None:
                    wait(dve, pv_done, T, a, T)
                    statistics(ln_att, a, lambda t: mix_bank[:, t * P:(t + 1) * P])
                if f is not None:
                    split_C(f, 2)
                    split_C(f, 3)

            dve.wait_ge(columns_loaded, 16)
            nc.vector.scalar_tensor_tensor(neg_wlr[:, :], columns[:, WL:WL + 1], -1.0, columns[:, WR:WR + 1],
                                           ALU.mult, ALU.mult).then_inc(neg_wlr_ready, 1)
            dve.wait_ge(neg_wlr_ready, 1)
            x_statistics(0)
            split_x(0)
            step(Stages(0))
            dve.wait_ge(w_hi_ready, 1)
            minus(w_lo[:, :], w_raw[:, :], w_hi[:, :].bitcast(f32)).then_inc(w_lo_ready, 1)
            nc.vector.memset(lo_count[:, 1:2], 0.0).then_inc(lo_counted, 1)
            dve.wait_ge(w_lo_ready, 1)
            nc.vector.tensor_scalar(w_raw[:, :], w_lo[:, :].bitcast(f32), 0.0, None, ALU.not_equal, ALU.add,
                                    accum_out=lo_count[:, 0:1]).then_inc(lo_counted, 1)
            dve.wait_ge(lo_summed, 1)
            nc.vector.tensor_copy(lo_total[:, :], eT_bank[:, 0:2]).then_inc(lo_known, 1)
            steps(dve, step, first=1)

        @block.gpsimd
        def _(pool):
            def rstd(norm, b, eps=None):
                mean, var = norm.mean_var[:, :, 0], norm.mean_var[:, :, 1]
                wait(pool, norm.mean_var_done, 1, b, 1, apart=True)
                if eps is None:
                    nc.gpsimd.tensor_scalar(norm.var_eps[:, :], var, EPS, 1.0, ALU.add, ALU.mult).then_inc(norm.chain, 1)
                else:
                    nc.gpsimd.tensor_tensor(norm.var_eps[:, :], var, eps, ALU.add).then_inc(norm.chain, 1)
                wait(pool, norm.chain, 4, b, 1)
                nc.gpsimd.tensor_tensor(norm.rstd[:, :], norm.var_eps[:, :], minus_half[:, :], ALU.pow).then_inc(norm.chain, 1)
                wait(pool, norm.chain, 4, b, 2)
                nc.gpsimd.tensor_tensor(norm.scaled_mean[:, :], mean, norm.rstd[:, :], ALU.mult).then_inc(norm.chain, 1)
                wait(pool, norm.chain, 4, b, 3, apart=True)
                nc.gpsimd.tensor_scalar(norm.shift[:, :], norm.scaled_mean[:, :], -1.0, 1.0, ALU.mult, ALU.mult).then_inc(norm.chain, 1)
                wait(pool, norm.chain, 4, b, 4, apart=True)

            def shifted(norm, src, out, done):
                for t in range(T):
                    op = nc.gpsimd.tensor_scalar(out[:, t, :], src[:, t, :], 1.0, norm.shift[:, t:t + 1], ALU.mult, ALU.add)
                op.then_inc(done, 1)

            def normalized(norm, src, out, done):
                for t in range(T):
                    op = nc.gpsimd.tensor_scalar(out[:, t, :], src[:, t, :], norm.rstd[:, t:t + 1],
                                                 norm.shift[:, t:t + 1], ALU.mult, ALU.add)
                op.then_inc(done, 1)

            def prepare(b):
                rstd(ln_x, b)
                wait(pool, xT_turned, 1, b, 0)
                wait(pool, xn_lo_ready, 1, b, 0, apart=True)
                normalized(ln_x, x_in, xn, xn_ready)

            def high_xn(b):
                wait(pool, xn_ready, 1, b, 1)
                wait(pool, pv_done, T, b, 0, apart=True)
                nc.gpsimd.tensor_copy(xn_hi[:, :, :], xn[:, :, :]).then_inc(xn_hi_ready, 1)

            def step(st):
                a, b, g = st.att, st.mid, st.tail
                if b is not None:
                    rstd(ln_x1, b)
                    wait(pool, x2T_turned, 1, b, 0, apart=True)
                    normalized(ln_x1, x1, x2n, x2n_ready)
                if a is not None:
                    high_xn(a)
                if g is not None:
                    rstd(ln_y, g)
                    wait(pool, x1_tail_loaded, 16, g, 16)
                    wait(pool, y_ready, 1, g, 0, apart=True)
                    shifted(ln_y, x1_tail, ffn_base, ffn_base_ready)
                if st.prep is not None:
                    prepare(st.prep)
                if a is not None:
                    wait(pool, exp_done, T, a, T)
                    nc.gpsimd.tensor_tensor(rs_squared[:, :], row_sum[:, :], row_sum[:, :], ALU.mult).then_inc(rs_chain, 1)
                    wait(pool, rs_chain, 2, a, 1, apart=True)
                    nc.gpsimd.tensor_scalar(rs_eps[:, :], rs_squared[:, :], EPS, 1.0, ALU.mult, ALU.mult).then_inc(rs_chain, 1)
                    wait(pool, rs_chain, 2, a, 2)
                    rstd(ln_att, a, rs_eps[:, :])
                    wait(pool, x_res_loaded, 16, a, 16)
                    wait(pool, x1_ready, 1, a, 0, apart=True)
                    shifted(ln_att, x_res, att_base, att_base_ready)

            nc.gpsimd.memset(ident[:, :], 0.0).then_inc(consts_zeroed, 1)
            nc.gpsimd.memset(minus_half[:, :], -0.5).then_inc(consts_zeroed, 1)
            nc.gpsimd.memset(ones[:, :], 1.0).then_inc(consts_ready, 1)
            pool.wait_ge(consts_zeroed, 2)
            nc.gpsimd.affine_select(out=ident[:, :], in_=ident[:, :], compare_op=ALU.not_equal, fill=1.0, base=0,
                                    pattern=[[-1, P]], channel_multiplier=1).then_inc(consts_ready, 1)
            prepare(0)
            steps(pool, step, first=0)


def kernel(L0_attn_x, L0_attn_w_lhs, L0_attn_w_rhs, L0_ffn_w1_w, L0_ffn_w1_s, L0_ffn_w2_w, L0_ffn_w2_s,
           L0_ffn_h1_w, L0_ffn_h1_s, L0_ffn_h2_w, L0_ffn_h2_s, L0_ffn_w3_w, L0_ffn_w3_s):
    import numpy as np
    import concourse.bacc as bacc
    from concourse.bass_utils import run_bass_kernel_spmd

    def tiles(w):
        w = np.asarray(w)
        return w.T.reshape(-1, 128, w.shape[0]).transpose(1, 0, 2).reshape(128, -1)

    def column(s):
        return np.asarray(s).reshape(-1, 128).T

    arrays = {
        "x_dram": np.ascontiguousarray(L0_attn_x),
        "weights_dram": np.concatenate(
            [tiles(w) for w in (L0_ffn_w1_w, L0_ffn_w2_w, L0_ffn_w3_w, L0_ffn_h1_w, L0_ffn_h2_w)], axis=1),
        "columns_dram": np.concatenate(
            [column(s) for s in (L0_ffn_w1_s, L0_ffn_w2_s, L0_ffn_h1_s, L0_ffn_h2_s, L0_ffn_w3_s,
                                 L0_attn_w_lhs, L0_attn_w_rhs)], axis=1),
    }
    nc = bacc.Bacc("TRN2", target_bir_lowering=False, num_devices=1)
    args = [nc.dram_tensor(n, a.shape, mybir.dt.from_np(a.dtype), kind="ExternalInput").ap() for n, a in arrays.items()]
    shape = arrays["x_dram"].shape
    args.append(nc.dram_tensor("out_dram", shape, mybir.dt.float32, kind="ExternalOutput").ap())
    sandwich_kernel(nc, *args)
    r = run_bass_kernel_spmd(nc, [arrays], core_ids=[0])
    return r.results[0]["out_dram"]
```

```python
from contextlib import ExitStack

import concourse.bass as bass
from concourse import mybir


def sandwich_kernel(
    nc: bass.Bass,
    x_dram: bass.AP,
    weights_dram: bass.AP,
    columns_dram: bass.AP,
    out_dram: bass.AP,
):
    f32, f32r, f16, i32 = mybir.dt.float32, mybir.dt.float32r, mybir.dt.float16, mybir.dt.int32
    ALU = mybir.AluOpType
    ACT = mybir.ActivationFunctionType
    AX = mybir.AxisListType

    N, S, D = x_dram.shape
    P = 128
    T = S // P
    K = (columns_dram.shape[1] - 3) // 4
    H = K * P
    W = weights_dram.shape[1]
    EPS = 1e-5
    W1, W2, W3 = 0, H, 2 * H
    H1, H2 = 3 * H, 3 * H + K * H
    WEIGHT_PARTS = [slice(W1, W3), slice(H1, H2), slice(H2, W), slice(W3, H1)]
    S1, S2, SH1, SH2, S3, WL, WR = 0, K, 2 * K, 3 * K, 4 * K, 4 * K + 1, 4 * K + 2

    with ExitStack() as ctx:
        def sb(name, shape, dt):
            return ctx.enter_context(nc.sbuf_tensor(name, shape, dt))

        def ps(name):
            return ctx.enter_context(nc.psum_tensor(name, [P, S], f32))

        def sem(name):
            return ctx.enter_context(nc.semaphore(name))

        ident = sb("ident", [P, P], f32)
        ones = sb("ones", [P, P], f32)
        minus_half = sb("minus_half", [P, T], f32)
        columns = sb("columns", [P, 4 * K + 3], f32)
        neg_wlr = sb("neg_wlr", [P, 1], f32)
        w_raw = sb("w_raw", [P, W], f32)
        w_hi = sb("w_hi", [P, W], f32r)
        w_lo = sb("w_lo", [P, W], f32r)
        lo_count = sb("lo_count", [P, len(WEIGHT_PARTS)], f32)
        lo_total = sb("lo_total", [P, 1], f32)
        x_in = sb("x_in", [P, T, D], f32)
        x_res = sb("x_res", [P, T, D], f32)
        xn = sb("xn", [P, T, D], f32)
        xn_hi = sb("xn_hi", [P, T, D], f16)
        xn_lo = sb("xn_lo", [P, T, D], f16)
        x1 = sb("x1", [P, T, D], f32)
        x1_all = sb("x1_all", [P, N, T * D], f32)
        x1_tail = sb("x1_tail", [P, T, D], f32)
        x2n = sb("x2n", [P, T, D], f32)
        att_base = sb("att_base", [P, T, D], f32)
        ffn_base = sb("ffn_base", [P, T, D], f32)
        y_out = sb("y_out", [P, T, D], f32)
        xT_hi = sb("xT_hi", [P, S], f32r)
        xT_lo = sb("xT_lo", [P, S], f32r)
        aT_hi = sb("aT_hi", [P, S], f32r)
        aT_lo = sb("aT_lo", [P, S], f32r)
        x2T_hi = sb("x2T_hi", [P, S], f32r)
        x2T_lo = sb("x2T_lo", [P, S], f32r)
        yT = sb("yT", [P, S], f32)
        neg_max = sb("neg_max", [P, T], f32)
        row_sum = sb("row_sum", [P, T], f32)
        exps = sb("exps", [P, T, S], f32)
        eT_hi = sb("eT_hi", [P, 2, T, P], f16)
        eT_lo = sb("eT_lo", [P, 2, T, P], f16)
        gate = sb("gate", [P, 2, S], f32)
        h_full = sb("h_full", [P, K, S], f32)
        hA_hi, hB_hi = (sb(f"h{c}_hi", [P, K, S], f32r) for c in "AB")
        hA_lo, hB_lo = (sb(f"h{c}_lo", [P, K, S], f32r) for c in "AB")
        hC_hi, hC_lo = hA_hi, hA_lo

        hid_bank = [ps(f"hid_bank{m}") for m in range(4)]
        score_bank = [ps(f"score_bank{m}") for m in range(2)]
        eT_bank = ps("eT_bank")
        mix_bank = ps("mix_bank")
        w3_bank = x2T_bank = eT_bank
        xT_bank = score_bank[0]
        y_bank = mix_bank

        x_loaded = sem("x_loaded")
        x_res_loaded = sem("x_res_loaded")
        w_loaded = [sem(f"w_loaded{c}") for c in range(len(WEIGHT_PARTS))]
        columns_loaded = sem("columns_loaded")
        out_stored = sem("out_stored")
        x1_saved, x1_tail_loaded = sem("x1_saved"), sem("x1_tail_loaded")
        consts_zeroed = sem("consts_zeroed")
        consts_ready = sem("consts_ready")
        w_hi_ready, w_lo_ready = sem("w_hi_ready"), sem("w_lo_ready")
        lo_counted, lo_summed, lo_known = sem("lo_counted"), sem("lo_summed"), sem("lo_known")
        neg_wlr_ready = sem("neg_wlr_ready")
        xT_turned, x2T_turned, y_turned = sem("xT_turned"), sem("x2T_turned"), sem("y_turned")
        scores_done, eT_turned, pv_done = sem("scores_done"), sem("eT_turned"), sem("pv_done")
        gated_mm, h1_mm, h2_mm = sem("gated_mm"), sem("h1_mm"), sem("h2_mm")
        w3_mm = sem("w3_mm")
        xT_hi_ready = sem("xT_hi_ready")
        exp_done, eT_hi_ready = sem("exp_done"), sem("eT_hi_ready")
        gate_ready, gelu1_done, gelu2_done = sem("gate_ready"), sem("gelu1_done"), sem("gelu2_done")
        yT_ready, x2T_hi_ready = sem("yT_ready"), sem("x2T_hi_ready")
        max_ready, eT_lo_ready = sem("max_ready"), sem("eT_lo_ready")
        gated_done = sem("gated_done")
        hA_lo_ready, hB_lo_ready, hC_lo_ready = (sem(f"h{c}_lo_ready") for c in "ABC")
        xT_lo_ready = sem("xT_lo_ready")
        x2T_lo_ready, xn_lo_ready = sem("x2T_lo_ready"), sem("xn_lo_ready")
        x1_ready, y_ready = sem("x1_ready"), sem("y_ready")
        hA_hi_ready = sem("hA_hi_ready")
        xn_ready, xn_hi_ready, x2n_ready = sem("xn_ready"), sem("xn_hi_ready"), sem("x2n_ready")
        att_base_ready, ffn_base_ready = sem("att_base_ready"), sem("ffn_base_ready")
        rs_chain = sem("rs_chain")

        waits_apart = sem("waits_apart")

        class Norm:
            def __init__(self, name):
                self.stats = sb(f"{name}_stats", [P, T, 6], f32)
                self.mean_var = sb(f"{name}_mean_var", [P, T, 2], f32)
                self.var_eps = sb(f"{name}_var_eps", [P, T], f32)
                self.rstd = sb(f"{name}_rstd", [P, T], f32)
                self.scaled_mean = sb(f"{name}_scaled_mean", [P, T], f32)
                self.shift = sb(f"{name}_shift", [P, T], f32)
                self.stats_done = sem(f"{name}_stats_done")
                self.mean_var_done = sem(f"{name}_mean_var_done")
                self.chain = sem(f"{name}_chain")

        ln_x, ln_att, ln_x1, ln_y = Norm("ln_x"), Norm("ln_att"), Norm("ln_x1"), Norm("ln_y")
        rs_squared = sb("rs_squared", [P, T], f32)
        rs_eps = sb("rs_eps", [P, T], f32)

        def apart(eng):
            eng.sem_inc(waits_apart, 1)

        def wait_free(eng, semaphore, per, b, count):
            if isinstance(b, int):
                if per * b + count > 0:
                    eng.wait_ge(semaphore, min(per * b + count, per * N))
            else:
                eng.wait_ge(semaphore, b * per + count)

        def x_view(dram, b):
            return dram[b, :, :].rearrange("(p t) d -> p t d", t=T)

        block = ctx.enter_context(nc.Block())

        class Stages:
            def __init__(self, i, full=False):
                def batch(b):
                    return b if full or 0 <= b < N else None
                self.prep, self.att, self.mid, self.ffn, self.tail = (batch(i + d) for d in (1, 0, -1, -2, -3))
                self.index = None if full else i

        def steps(eng, step, first=2):
            for i in range(first, 4):
                step(Stages(i))
            with eng.Fori(4, N - 1) as i:
                step(Stages(i, full=True))
            for i in range(N - 1, N + 3):
                step(Stages(i))

        @block.sync
        def _(sp):
            def load_x(b):
                wait_free(sp, xn_ready, 1, b, 0)
                sp.dma_start(x_in[:, :, :], x_view(x_dram, b)).then_inc(x_loaded, 16)

            def load_x_res(a):
                wait_free(sp, att_base_ready, 1, a, 0)
                sp.dma_start(x_res[:, :, :], x_view(x_dram, a)).then_inc(x_res_loaded, 16)

            def save_x1(b):
                sp.wait_ge(x1_ready, b + 1)
                sp.dma_start(x1_all[:, b, :], x1[:, :, :].rearrange("p t d -> p (t d)")).then_inc(x1_saved, 16)

            def load_x1_tail(g):
                sp.wait_ge(x1_saved, g * 16 + 16)
                wait_free(sp, ffn_base_ready, 1, g, 0)
                sp.dma_start(x1_tail[:, :, :].rearrange("p t d -> p (t d)"), x1_all[:, g, :]).then_inc(x1_tail_loaded, 16)

            def store(g):
                sp.wait_ge(y_ready, g + 1)
                sp.dma_start(x_view(out_dram, g), y_out[:, :, :]).then_inc(out_stored, 16)

            def step(st):
                a, b, g = st.att, st.mid, st.tail
                if st.prep is not None:
                    load_x(st.prep)
                if g is not None:
                    load_x1_tail(g)
                    store(g)
                if b is not None:
                    save_x1(b)
                if a is not None:
                    load_x_res(a)

            load_x(0)
            sp.dma_start(columns[:, :], columns_dram).then_inc(columns_loaded, 16)
            for c, part in enumerate(WEIGHT_PARTS):
                sp.dma_start(w_raw[:, part], weights_dram[:, part]).then_inc(w_loaded[c], 16)
            steps(sp, step, first=0)
            sp.wait_ge(out_stored, 16 * N)

        @block.tensor
        def _(pe):
            def matmuls(out, pairs):
                for n, (lhs, rhs) in enumerate(pairs):
                    mm = nc.tensor.matmul(out, lhs, rhs, start=(n == 0), stop=(n == len(pairs) - 1))
                return mm

            def turn(bank, src, done):
                for t in range(T):
                    mm = nc.tensor.transpose(bank[:, t * P:(t + 1) * P], src[:, t * P:(t + 1) * P], ident[:, :])
                mm.then_inc(done, 1)

            def turn_x(b):
                pe.wait_ge(xn_ready, b + 1)
                wait_free(pe, exp_done, T, b, -1)
                turn(xT_bank, xn[:, :, :].rearrange("p t d -> p (t d)"), xT_turned)

            def scores(b, j):
                if j == 0:
                    pe.wait_ge(xT_lo_ready, b * 2 + 2)
                wait_free(pe, exp_done, T, b, j - 1)
                rows = slice(j * P, (j + 1) * P)
                matmuls(score_bank[j % 2][:, :], [
                    (aT_hi[:, rows], xT_hi[:, :]), (aT_hi[:, rows], xT_lo[:, :]), (aT_lo[:, rows], xT_hi[:, :]),
                ]).then_inc(scores_done, 1)

            def turn_e(b, j):
                pe.wait_ge(exp_done, b * T + j + 1)
                if j == 0:
                    wait_free(pe, x2T_lo_ready, 1, b, 0)
                wait_free(pe, eT_lo_ready, T, b, j)
                turn(eT_bank, exps[:, j, :], eT_turned)

            def attend(b, j):
                if j == 0:
                    pe.wait_ge(xn_lo_ready, b + 1)
                    wait_free(pe, y_ready, 1, b, -2)
                    wait_free(pe, x1_ready, 1, b, 0)
                pe.wait_ge(eT_lo_ready, b * T + j + 1)
                pairs = []
                for t in range(T):
                    hi, lo = eT_hi[:, j % 2, t, :], eT_lo[:, j % 2, t, :]
                    pairs += [(hi, xn_hi[:, t, :]), (hi, xn_lo[:, t, :]), (lo, xn_hi[:, t, :])]
                matmuls(mix_bank[:, j * P:(j + 1) * P], pairs).then_inc(pv_done, 1)

            def turn_x2(b):
                pe.wait_ge(x2n_ready, b + 1)
                wait_free(pe, yT_ready, 1, b, -1)
                turn(x2T_bank, x2n[:, :, :].rearrange("p t d -> p (t d)"), x2T_turned)

            def products(general, col, hi, lo):
                w = slice(col, col + P)
                pairs = [(w_hi[:, w], hi), (w_hi[:, w], lo)]
                return pairs + ([(w_lo[:, w], hi)] if general else [])

            def gated(general, b, m):
                if m == 0:
                    pe.wait_ge(x2T_lo_ready, b + 1)
                if m < 2:
                    wait_free(pe, gelu2_done, K, b, 2 * m + 2 - K)
                else:
                    wait_free(pe, gated_done, K, b, m - 1)
                for bank, w in ((hid_bank[2 * (m % 2)], W1), (hid_bank[2 * (m % 2) + 1], W2)):
                    mm = matmuls(bank[:, :], products(general, w + m * P, x2T_hi[:, :], x2T_lo[:, :]))
                mm.then_inc(gated_mm, 1)

            def hidden(general, b, tiles, ks, w, hi, lo, lo_ready, bank_read, tiles_read, done):
                for m in tiles:
                    if 0 in ks:
                        pe.wait_ge(bank_read, b * K + tiles_read(m))
                    for k in ks:
                        if m == 0:
                            pe.wait_ge(lo_ready, b * K + k + 1)
                        pairs = products(general, w + k * H + m * P, hi[:, k, :], lo[:, k, :])
                        for n, (lhs, rhs) in enumerate(pairs):
                            mm = nc.tensor.matmul(hid_bank[m][:, :], lhs, rhs, start=(k == 0 and n == 0),
                                                  stop=(k == K - 1 and n == len(pairs) - 1))
                    if K - 1 in ks:
                        mm.then_inc(done, 1)

            def layer1(general, b, tiles, ks):
                hidden(general, b, tiles, ks, H1, hA_hi, hA_lo, hA_lo_ready,
                       gated_done, lambda m: 3 + m // 2, h1_mm)

            def layer2(general, b, tiles, ks):
                hidden(general, b, tiles, ks, H2, hB_hi, hB_lo, hB_lo_ready,
                       gelu1_done, lambda m: m + 1, h2_mm)

            def layer3(general, b, ks):
                if 0 in ks:
                    wait_free(pe, eT_lo_ready, T, b, 3 * T)
                for k in ks:
                    pe.wait_ge(hC_lo_ready, b * K + k + 1)
                    pairs = products(general, W3 + k * P, hC_hi[:, k, :], hC_lo[:, k, :])
                    for n, (lhs, rhs) in enumerate(pairs):
                        mm = nc.tensor.matmul(w3_bank[:, :], lhs, rhs, start=(k == 0 and n == 0),
                                              stop=(k == K - 1 and n == len(pairs) - 1))
                if K - 1 in ks:
                    mm.then_inc(w3_mm, 1)

            def turn_y(b):
                pe.wait_ge(yT_ready, b + 1)
                wait_free(pe, x1_ready, 1, b, 3)
                turn(y_bank, yT, y_turned)

            def sum_counts():
                pe.wait_ge(lo_counted, len(WEIGHT_PARTS))
                nc.tensor.matmul(hid_bank[0][:, 0:len(WEIGHT_PARTS)], ones[:, :], lo_count[:, :], start=True,
                                 stop=True).then_inc(lo_summed, 1)

            def make_step(general):
                def step(st):
                    a, f, g = st.att, st.ffn, st.tail
                    if f is not None:
                        gated(general, f, 0)
                    if g is not None:
                        layer3(general, g, (0,))
                    if a is not None:
                        scores(a, 0)
                    if f is not None:
                        gated(general, f, 1)
                    if g is not None:
                        layer3(general, g, (1, 2, 3))
                    if f is not None:
                        gated(general, f, 2)
                        gated(general, f, 3)
                    if g is not None:
                        turn_y(g)
                    if a is not None:
                        scores(a, 1)
                    if f is not None:
                        layer1(general, f, (0,), (0,))
                    if a is not None:
                        scores(a, 2)
                    if f is not None:
                        layer1(general, f, (1,), (0,))
                    if a is not None:
                        scores(a, 3)
                    if f is not None:
                        layer1(general, f, (2,), (0,))
                        layer1(general, f, (0,), (1,))
                        layer1(general, f, (3,), (0,))
                        layer1(general, f, (1, 3), (1,))
                    if st.mid is not None:
                        turn_x2(st.mid)
                    if f is not None:
                        layer1(general, f, (0,), (2,))
                        layer1(general, f, (2,), (1,))
                        layer1(general, f, (1,), (2,))
                        layer1(general, f, (0,), (3,))
                        layer1(general, f, (2,), (2,))
                    if a is not None:
                        turn_e(a, 0)
                    if f is not None:
                        layer1(general, f, (1,), (3,))
                        layer1(general, f, (3,), (2,))
                        layer1(general, f, (2, 3), (3,))
                        layer2(general, f, (0,), (0,))
                    if a is not None:
                        turn_e(a, 1)
                    if st.prep is not None:
                        turn_x(st.prep)
                    if f is not None:
                        layer2(general, f, (1,), (0,))
                        layer2(general, f, (0,), (1,))
                        layer2(general, f, (2,), (0,))
                        layer2(general, f, (1,), (1,))
                        layer2(general, f, (0,), (2,))
                        layer2(general, f, (2,), (1,))
                        layer2(general, f, (1,), (2,))
                        layer2(general, f, (0,), (3,))
                        layer2(general, f, (3,), (0,))
                    if a is not None:
                        attend(a, 0)
                        turn_e(a, 2)
                        attend(a, 1)
                    if f is not None:
                        layer2(general, f, (1,), (3,))
                        layer2(general, f, (2,), (2,))
                        layer2(general, f, (3,), (1,))
                    if a is not None:
                        turn_e(a, 3)
                    if f is not None:
                        layer2(general, f, (2,), (3,))
                        layer2(general, f, (3,), (2,))
                    if a is not None:
                        attend(a, 2)
                    if st.index == 1:
                        sum_counts()
                    if f is not None:
                        layer2(general, f, (3,), (3,))
                    if a is not None:
                        attend(a, 3)
                return step

            pe.wait_ge(consts_ready, 2)
            turn_x(0)
            common = make_step(False)
            common(Stages(0))
            common(Stages(1))
            pe.wait_ge(lo_known, 1)
            any_lo = pe.value_load(lo_total[0:1, 0:1].bitcast(i32))
            with pe.If(any_lo != 0):
                steps(pe, make_step(True))
            with pe.Else():
                steps(pe, make_step(False))

        @block.scalar
        def _(act):
            def high_xT(b):
                act.wait_ge(xT_turned, b + 1)
                wait_free(act, scores_done, T, b, 0)
                nc.scalar.copy(xT_hi[:, :], xT_bank[:, :]).then_inc(xT_hi_ready, 1)

            def high_aT(b):
                nc.scalar.mul(aT_hi[:, :], xT_bank[:, :], neg_wlr[:, 0:1]).then_inc(xT_hi_ready, 1)

            def softmax(b, j):
                act.wait_ge(max_ready, b * T + j + 1)
                wait_free(act, eT_turned, T, b, j + 1 - T)
                if j == 0:
                    wait_free(act, rs_chain, 2, b, -1)
                nc.scalar.activation(exps[:, j, :], score_bank[j % 2][:, :], ACT.Exp, bias=neg_max[:, j:j + 1],
                                     scale=-1.0, accum_out=row_sum[:, j:j + 1]).then_inc(exp_done, 1)

            def high_e(b, j):
                act.wait_ge(eT_turned, b * T + j + 1)
                wait_free(act, pv_done, T, b, j - 1)
                nc.scalar.copy(eT_hi[:, j % 2, :, :].rearrange("p t s -> p (t s)"), eT_bank[:, :]).then_inc(eT_hi_ready, 1)

            def silu(b, m):
                act.wait_ge(gated_mm, b * K + m + 1)
                wait_free(act, gated_done, K, b, m - 1)
                nc.scalar.activation(gate[:, m % 2, :], hid_bank[2 * (m % 2)][:, :], ACT.Silu,
                                     scale=columns[:, S1 + m:S1 + m + 1]).then_inc(gate_ready, 1)

            def gelu(b, m, mm, col, last_lo, hi, hi_used, per, count, done):
                act.wait_ge(mm, b * K + m + 1)
                act.wait_ge(last_lo, b * K + m + 1)
                if m == 0:
                    wait_free(act, hi_used, per, b, count)
                scale = columns[:, col + m:col + m + 1]
                nc.scalar.activation(h_full[:, m, :], hid_bank[m][:, :], ACT.Gelu, scale=scale)
                nc.scalar.activation(hi[:, m, :], hid_bank[m][:, :], ACT.Gelu, scale=scale).then_inc(done, 1)

            def gelu1(b, m):
                gelu(b, m, h1_mm, SH1, hA_lo_ready, hB_hi, h2_mm, K, 0, gelu1_done)

            def gelu2(b, m):
                gelu(b, m, h2_mm, SH2, hB_lo_ready, hC_hi, h1_mm, K, K, gelu2_done)

            def scale_y(b):
                act.wait_ge(w3_mm, b + 1)
                wait_free(act, y_turned, 1, b, 0)
                nc.scalar.mul(yT[:, :], w3_bank[:, :], columns[:, S3:S3 + 1]).then_inc(yT_ready, 1)

            def high_x2T(b):
                act.wait_ge(x2T_turned, b + 1)
                wait_free(act, gated_mm, K, b, 0)
                nc.scalar.copy(x2T_hi[:, :], x2T_bank[:, :]).then_inc(x2T_hi_ready, 1)

            def high_weights(c):
                part = WEIGHT_PARTS[c]
                act.wait_ge(w_loaded[c], 16)
                nc.scalar.copy(w_hi[:, part], w_raw[:, part]).then_inc(w_hi_ready, 1)

            def step(st):
                a, b, f, g = st.att, st.mid, st.ffn, st.tail
                if f is not None:
                    silu(f, 0)
                    silu(f, 1)
                if g is not None:
                    scale_y(g)
                if f is not None:
                    silu(f, 2)
                    silu(f, 3)
                if a is not None:
                    softmax(a, 0)
                    softmax(a, 1)
                if st.index == 1:
                    high_weights(3)
                if st.index == 0:
                    high_weights(0)
                if a is not None:
                    softmax(a, 2)
                    softmax(a, 3)
                if b is not None:
                    high_x2T(b)
                if f is not None:
                    gelu1(f, 0)
                if a is not None:
                    high_e(a, 0)
                if f is not None:
                    gelu1(f, 1)
                    gelu1(f, 2)
                    gelu1(f, 3)
                if a is not None:
                    high_e(a, 1)
                if st.prep is not None:
                    high_xT(st.prep)
                    high_aT(st.prep)
                if f is not None:
                    gelu2(f, 0)
                if a is not None:
                    high_e(a, 2)
                if f is not None:
                    gelu2(f, 1)
                if st.index == 0:
                    high_weights(1)
                if a is not None:
                    high_e(a, 3)
                if st.index == 0:
                    high_weights(2)
                if f is not None:
                    gelu2(f, 2)
                    gelu2(f, 3)

            act.wait_ge(columns_loaded, 16)
            act.wait_ge(neg_wlr_ready, 1)
            high_xT(0)
            high_aT(0)
            steps(act, step, first=0)

        @block.vector
        def _(dve):
            def minus(out, a, b):
                return nc.vector.tensor_tensor(out, a, b, ALU.subtract)

            def statistics(norm, tile):
                for t in range(T):
                    op = nc.vector.bn_stats(norm.stats[:, t, :], tile(t))
                op.then_inc(norm.stats_done, 1)

            def aggregate(norm, b):
                dve.wait_ge(norm.stats_done, b + 1)
                apart(dve)
                for t in range(T):
                    op = nc.vector.bn_aggr(norm.mean_var[:, t, :], norm.stats[:, t, :])
                op.then_inc(norm.mean_var_done, 1)

            def row_max(b, j):
                dve.wait_ge(scores_done, b * T + j + 1)
                nc.vector.tensor_reduce(neg_max[:, j:j + 1], score_bank[j % 2][:, :], AX.X, ALU.min).then_inc(max_ready, 1)

            def low_e(b, j):
                dve.wait_ge(eT_hi_ready, b * T + j + 1)
                minus(eT_lo[:, j % 2, :, :].rearrange("p t s -> p (t s)"), eT_bank[:, :],
                      eT_hi[:, j % 2, :, :].rearrange("p t s -> p (t s)")).then_inc(eT_lo_ready, 1)

            def gated(b, m):
                wait_free(dve, hC_lo_ready, K, b, m + 1 - K)
                dve.wait_ge(gate_ready, b * K + m + 1)
                nc.vector.scalar_tensor_tensor(h_full[:, m, :], hid_bank[2 * (m % 2) + 1][:, :],
                                               columns[:, S2 + m:S2 + m + 1], gate[:, m % 2, :],
                                               ALU.mult, ALU.mult).then_inc(gated_done, 1)

            def high_A(b, m):
                if m == 0:
                    wait_free(dve, w3_mm, 1, b, 0)
                dve.wait_ge(gated_done, b * K + m + 1)
                nc.vector.tensor_copy(hA_hi[:, m, :], h_full[:, m, :]).then_inc(hA_hi_ready, 1)

            def split_h(b, m, hi_ready, hi, lo, lo_ready):
                dve.wait_ge(hi_ready, b * K + m + 1)
                minus(lo[:, m, :], h_full[:, m, :], hi[:, m, :].bitcast(f32)).then_inc(lo_ready, 1)

            def low_A(b, m):
                split_h(b, m, hA_hi_ready, hA_hi, hA_lo, hA_lo_ready)

            def low_B(b, m):
                split_h(b, m, gelu1_done, hB_hi, hB_lo, hB_lo_ready)

            def low_C(b, m):
                split_h(b, m, gelu2_done, hC_hi, hC_lo, hC_lo_ready)

            def x_statistics(b):
                dve.wait_ge(x_loaded, b * 16 + 16)
                statistics(ln_x, lambda t: x_in[:, t, :])

            def low_xn(b):
                dve.wait_ge(xn_hi_ready, b + 1)
                minus(xn_lo[:, :, :], xn[:, :, :], xn_hi[:, :, :]).then_inc(xn_lo_ready, 1)

            def low_xT(b):
                dve.wait_ge(xT_hi_ready, b * 2 + 2)
                minus(xT_lo[:, :], xT_bank[:, :], xT_hi[:, :].bitcast(f32)).then_inc(xT_lo_ready, 1)

            def low_aT(b):
                dve.wait_ge(xT_hi_ready, b * 2 + 2)
                nc.vector.scalar_tensor_tensor(aT_lo[:, :], xT_bank[:, :], neg_wlr[:, 0:1], aT_hi[:, :].bitcast(f32),
                                               ALU.mult, ALU.subtract).then_inc(xT_lo_ready, 1)

            def scaled_add(norm, b, src, base, base_ready, out, done):
                dve.wait_ge(base_ready, b + 1)
                for t in range(T):
                    op = nc.vector.scalar_tensor_tensor(out[:, t, :], src[:, t * P:(t + 1) * P], norm.rstd[:, t:t + 1],
                                                        base[:, t, :], ALU.mult, ALU.add)
                op.then_inc(done, 1)

            def add_attention(b):
                wait_free(dve, x1_saved, 16, b, 0)
                wait_free(dve, x2n_ready, 1, b, 0)
                scaled_add(ln_att, b, mix_bank, att_base, att_base_ready, x1, x1_ready)

            def x1_statistics(b):
                dve.wait_ge(x1_ready, b + 1)
                statistics(ln_x1, lambda t: x1[:, t, :])

            def low_x2T(b):
                dve.wait_ge(x2T_hi_ready, b + 1)
                minus(x2T_lo[:, :], x2T_bank[:, :], x2T_hi[:, :].bitcast(f32)).then_inc(x2T_lo_ready, 1)

            def y_statistics(b):
                dve.wait_ge(y_turned, b + 1)
                statistics(ln_y, lambda t: y_bank[:, t * P:(t + 1) * P])

            def add_ffn(b):
                wait_free(dve, out_stored, 16, b, 0)
                scaled_add(ln_y, b, y_bank, ffn_base, ffn_base_ready, y_out, y_ready)

            def attention_statistics(b):
                dve.wait_ge(pv_done, b * T + T)
                statistics(ln_att, lambda t: mix_bank[:, t * P:(t + 1) * P])

            def low_weights(c):
                part = WEIGHT_PARTS[c]
                dve.wait_ge(w_hi_ready, c + 1)
                minus(w_lo[:, part], w_raw[:, part], w_hi[:, part].bitcast(f32)).then_inc(w_lo_ready, 1)

            def count_lo(c):
                part = WEIGHT_PARTS[c]
                dve.wait_ge(w_lo_ready, c + 1)
                nc.vector.tensor_scalar(w_raw[:, part], w_lo[:, part].bitcast(f32), 0.0, None, ALU.not_equal, ALU.add,
                                        accum_out=lo_count[:, c:c + 1]).then_inc(lo_counted, 1)

            def total_count():
                dve.wait_ge(lo_summed, 1)
                nc.vector.tensor_reduce(lo_total[:, :], hid_bank[0][:, 0:len(WEIGHT_PARTS)], AX.X, ALU.add).then_inc(lo_known, 1)

            def step(st):
                a, b, f, g = st.att, st.mid, st.ffn, st.tail
                if a is not None:
                    row_max(a, 0)
                if f is not None:
                    gated(f, 0)
                if st.prep is not None:
                    x_statistics(st.prep)
                if f is not None:
                    gated(f, 1)
                    high_A(f, 0)
                if b is not None:
                    add_attention(b)
                if f is not None:
                    gated(f, 2)
                if b is not None:
                    x1_statistics(b)
                if f is not None:
                    low_A(f, 0)
                if b is not None:
                    aggregate(ln_x1, b)
                if a is not None:
                    row_max(a, 1)
                if f is not None:
                    high_A(f, 1)
                    gated(f, 3)
                    low_A(f, 1)
                    high_A(f, 2)
                if a is not None:
                    row_max(a, 2)
                if st.prep is not None:
                    aggregate(ln_x, st.prep)
                if a is not None:
                    row_max(a, 3)
                if st.index == 1:
                    count_lo(1)
                if f is not None:
                    low_A(f, 2)
                    high_A(f, 3)
                    low_A(f, 3)
                if b is not None:
                    low_x2T(b)
                if st.index == 1:
                    low_weights(3)
                if a is not None:
                    low_xn(a)
                if g is not None:
                    y_statistics(g)
                    aggregate(ln_y, g)
                if f is not None:
                    low_B(f, 0)
                if a is not None:
                    low_e(a, 0)
                if st.index == 0:
                    low_weights(0)
                if f is not None:
                    low_B(f, 1)
                    low_B(f, 2)
                    low_B(f, 3)
                if g is not None:
                    add_ffn(g)
                if st.index == 1:
                    count_lo(2)
                if a is not None:
                    low_e(a, 1)
                if st.prep is not None:
                    low_xT(st.prep)
                    low_aT(st.prep)
                if a is not None:
                    low_e(a, 2)
                if st.index == 1:
                    count_lo(3)
                if st.index == 0:
                    count_lo(0)
                if f is not None:
                    low_C(f, 0)
                    low_C(f, 1)
                if a is not None:
                    low_e(a, 3)
                if st.index == 1:
                    total_count()
                if st.index == 0:
                    low_weights(1)
                if f is not None:
                    low_C(f, 2)
                if a is not None:
                    attention_statistics(a)
                    aggregate(ln_att, a)
                if st.index == 0:
                    low_weights(2)
                if f is not None:
                    low_C(f, 3)

            dve.wait_ge(columns_loaded, 16)
            nc.vector.scalar_tensor_tensor(neg_wlr[:, :], columns[:, WL:WL + 1], -1.0, columns[:, WR:WR + 1],
                                           ALU.mult, ALU.mult).then_inc(neg_wlr_ready, 1)
            x_statistics(0)
            aggregate(ln_x, 0)
            dve.wait_ge(neg_wlr_ready, 1)
            low_xT(0)
            low_aT(0)
            steps(dve, step, first=0)

        @block.gpsimd
        def _(pool):
            def rstd(norm, b, eps=None):
                mean, var = norm.mean_var[:, :, 0], norm.mean_var[:, :, 1]
                pool.wait_ge(norm.mean_var_done, b + 1)
                apart(pool)
                if eps is None:
                    nc.gpsimd.tensor_scalar(norm.var_eps[:, :], var, EPS, 1.0, ALU.add, ALU.mult).then_inc(norm.chain, 1)
                else:
                    nc.gpsimd.tensor_tensor(norm.var_eps[:, :], var, eps, ALU.add).then_inc(norm.chain, 1)
                pool.wait_ge(norm.chain, b * 4 + 1)
                nc.gpsimd.tensor_tensor(norm.rstd[:, :], norm.var_eps[:, :], minus_half[:, :], ALU.pow).then_inc(norm.chain, 1)
                pool.wait_ge(norm.chain, b * 4 + 2)
                nc.gpsimd.tensor_tensor(norm.scaled_mean[:, :], mean, norm.rstd[:, :], ALU.mult).then_inc(norm.chain, 1)
                pool.wait_ge(norm.chain, b * 4 + 3)
                apart(pool)
                nc.gpsimd.tensor_scalar(norm.shift[:, :], norm.scaled_mean[:, :], -1.0, 1.0, ALU.mult, ALU.mult).then_inc(norm.chain, 1)
                pool.wait_ge(norm.chain, b * 4 + 4)
                apart(pool)

            def shifted(norm, src, out, done):
                for t in range(T):
                    op = nc.gpsimd.tensor_scalar(out[:, t, :], src[:, t, :], 1.0, norm.shift[:, t:t + 1], ALU.mult, ALU.add)
                op.then_inc(done, 1)

            def normalized(norm, src, out, done):
                for t in range(T):
                    op = nc.gpsimd.tensor_scalar(out[:, t, :], src[:, t, :], norm.rstd[:, t:t + 1],
                                                 norm.shift[:, t:t + 1], ALU.mult, ALU.add)
                op.then_inc(done, 1)

            def normalize_x(b):
                wait_free(pool, xT_turned, 1, b, 0)
                wait_free(pool, xn_lo_ready, 1, b, 0)
                apart(pool)
                normalized(ln_x, x_in, xn, xn_ready)

            def high_xn(b):
                pool.wait_ge(xn_ready, b + 1)
                wait_free(pool, pv_done, T, b, 0)
                apart(pool)
                nc.gpsimd.tensor_copy(xn_hi[:, :, :], xn[:, :, :]).then_inc(xn_hi_ready, 1)

            def normalize_x1(b):
                wait_free(pool, x2T_turned, 1, b, 0)
                apart(pool)
                normalized(ln_x1, x1, x2n, x2n_ready)

            def shift_x1(b):
                pool.wait_ge(x1_tail_loaded, b * 16 + 16)
                wait_free(pool, y_ready, 1, b, 0)
                apart(pool)
                shifted(ln_y, x1_tail, ffn_base, ffn_base_ready)

            def scaled_eps(b):
                pool.wait_ge(exp_done, b * T + T)
                nc.gpsimd.tensor_tensor(rs_squared[:, :], row_sum[:, :], row_sum[:, :], ALU.mult).then_inc(rs_chain, 1)
                pool.wait_ge(rs_chain, b * 2 + 1)
                apart(pool)
                nc.gpsimd.tensor_scalar(rs_eps[:, :], rs_squared[:, :], EPS, 1.0, ALU.mult, ALU.mult).then_inc(rs_chain, 1)
                pool.wait_ge(rs_chain, b * 2 + 2)

            def shift_x(b):
                pool.wait_ge(x_res_loaded, b * 16 + 16)
                wait_free(pool, x1_ready, 1, b, 0)
                apart(pool)
                shifted(ln_att, x_res, att_base, att_base_ready)

            def step(st):
                a, b, g = st.att, st.mid, st.tail
                if a is not None:
                    high_xn(a)
                if b is not None:
                    rstd(ln_x1, b)
                    normalize_x1(b)
                if st.prep is not None:
                    rstd(ln_x, st.prep)
                    normalize_x(st.prep)
                if g is not None:
                    rstd(ln_y, g)
                    shift_x1(g)
                if a is not None:
                    scaled_eps(a)
                    rstd(ln_att, a, rs_eps[:, :])
                    shift_x(a)

            nc.gpsimd.memset(ident[:, :], 0.0).then_inc(consts_zeroed, 1)
            nc.gpsimd.memset(minus_half[:, :], -0.5).then_inc(consts_zeroed, 1)
            nc.gpsimd.memset(ones[:, :], 1.0).then_inc(consts_ready, 1)
            pool.wait_ge(consts_zeroed, 2)
            nc.gpsimd.affine_select(out=ident[:, :], in_=ident[:, :], compare_op=ALU.not_equal, fill=1.0, base=0,
                                    pattern=[[-1, P]], channel_multiplier=1).then_inc(consts_ready, 1)
            rstd(ln_x, 0)
            normalize_x(0)
            steps(pool, step, first=0)


def kernel(L0_attn_x, L0_attn_w_lhs, L0_attn_w_rhs, L0_ffn_w1_w, L0_ffn_w1_s, L0_ffn_w2_w, L0_ffn_w2_s,
           L0_ffn_h1_w, L0_ffn_h1_s, L0_ffn_h2_w, L0_ffn_h2_s, L0_ffn_w3_w, L0_ffn_w3_s):
    import numpy as np
    import concourse.bacc as bacc
    from concourse.bass_utils import run_bass_kernel_spmd

    def tiles(w):
        w = np.asarray(w)
        return w.T.reshape(-1, 128, w.shape[0]).transpose(1, 0, 2).reshape(128, -1)

    def column(s):
        return np.asarray(s).reshape(-1, 128).T

    arrays = {
        "x_dram": np.ascontiguousarray(L0_attn_x),
        "weights_dram": np.concatenate(
            [tiles(w) for w in (L0_ffn_w1_w, L0_ffn_w2_w, L0_ffn_w3_w, L0_ffn_h1_w, L0_ffn_h2_w)], axis=1),
        "columns_dram": np.concatenate(
            [column(s) for s in (L0_ffn_w1_s, L0_ffn_w2_s, L0_ffn_h1_s, L0_ffn_h2_s, L0_ffn_w3_s,
                                 L0_attn_w_lhs, L0_attn_w_rhs)], axis=1),
    }
    nc = bacc.Bacc("TRN2", target_bir_lowering=False, num_devices=1)
    args = [nc.dram_tensor(n, a.shape, mybir.dt.from_np(a.dtype), kind="ExternalInput").ap() for n, a in arrays.items()]
    shape = arrays["x_dram"].shape
    args.append(nc.dram_tensor("out_dram", shape, mybir.dt.float32, kind="ExternalOutput").ap())
    sandwich_kernel(nc, *args)
    r = run_bass_kernel_spmd(nc, [arrays], core_ids=[0])
    return r.results[0]["out_dram"]
```

```python
from contextlib import ExitStack

import concourse.bass as bass
from concourse import mybir


def sandwich_kernel(
    nc: bass.Bass,
    x_dram: bass.AP,
    weights_dram: bass.AP,
    columns_dram: bass.AP,
    out_dram: bass.AP,
):
    f32, f32r, f16, i32 = mybir.dt.float32, mybir.dt.float32r, mybir.dt.float16, mybir.dt.int32
    ALU = mybir.AluOpType
    ACT = mybir.ActivationFunctionType
    AX = mybir.AxisListType

    N, S, D = x_dram.shape
    P = 128
    T = S // P
    K = (columns_dram.shape[1] - 3) // 4
    H = K * P
    W = weights_dram.shape[1]
    EPS = 1e-5
    W1, W2, W3 = 0, H, 2 * H
    H1, H2 = 3 * H, 3 * H + K * H
    WEIGHT_PARTS = [slice(W1, W3), slice(H1, (H1 + H2) // 2), slice((H1 + H2) // 2, H2),
                    slice(H2, (H2 + W) // 2), slice((H2 + W) // 2, W), slice(W3, H1)]
    S1, S2, SH1, SH2, S3, WL, WR = 0, K, 2 * K, 3 * K, 4 * K, 4 * K + 1, 4 * K + 2

    with ExitStack() as ctx:
        def sb(name, shape, dt):
            return ctx.enter_context(nc.sbuf_tensor(name, shape, dt))

        def ps(name):
            return ctx.enter_context(nc.psum_tensor(name, [P, S], f32))

        def sem(name):
            return ctx.enter_context(nc.semaphore(name))

        ident = sb("ident", [P, P], f32)
        ones = sb("ones", [P, P], f32)
        table_loader = sb("table_loader", [P, 1], f32)
        minus_half = sb("minus_half", [P, T], f32)
        columns = sb("columns", [P, 4 * K + 3], f32)
        neg_wlr = sb("neg_wlr", [P, 1], f32)
        w_raw = sb("w_raw", [P, W], f32)
        w_hi = sb("w_hi", [P, W], f32r)
        w_lo = sb("w_lo", [P, W], f32r)
        lo_sum = sb("lo_sum", [P, len(WEIGHT_PARTS)], f32)
        lo_total = sb("lo_total", [P, 1], f32)
        x_in = sb("x_in", [P, T, D], f32)
        x_res = sb("x_res", [P, T, D], f32)
        xn = sb("xn", [P, T, D], f32)
        xn_hi = sb("xn_hi", [P, T, D], f16)
        xn_lo = sb("xn_lo", [P, T, D], f16)
        x1 = sb("x1", [P, T, D], f32)
        x1_all = sb("x1_all", [P, N, T * D], f32)
        x1_tail = sb("x1_tail", [P, T, D], f32)
        x2n = sb("x2n", [P, T, D], f32)
        att_base = sb("att_base", [P, T, D], f32)
        xT_hi = sb("xT_hi", [P, S], f32r)
        xT_lo = sb("xT_lo", [P, S], f32r)
        aT_hi = sb("aT_hi", [P, S], f32r)
        aT_lo = sb("aT_lo", [P, S], f32r)
        x2T_hi = sb("x2T_hi", [P, S], f32r)
        x2T_lo = sb("x2T_lo", [P, S], f32r)
        neg_max = sb("neg_max", [P, T], f32)
        row_sum = sb("row_sum", [P, T], f32)
        exps = sb("exps", [P, T, S], f32)
        eT_hi = sb("eT_hi", [P, T, T, P], f16)
        eT_lo = sb("eT_lo", [P, T, T, P], f16)
        hA_hi, hB_hi, hC_hi = (sb(f"h{c}_hi", [P, K, S], f32r) for c in "ABC")
        hA_lo, hB_lo, hC_lo = (sb(f"h{c}_lo", [P, K, S], f32r) for c in "ABC")
        h_full = w_raw[:, 0:K * S].rearrange("p (k s) -> p k s", k=K)
        gate = w_raw[:, K * S:(K + 2) * S].rearrange("p (k s) -> p k s", k=2)
        yT = w_raw[:, (K + 2) * S:(K + 3) * S]
        ffn_base, y_out = (w_raw[:, n * S:(n + 1) * S].rearrange("p (t d) -> p t d", t=T) for n in (K + 3, K + 4))

        hid_bank = [ps(f"hid_bank{m}") for m in range(4)]
        score_bank = [ps(f"score_bank{m}") for m in range(2)]
        eT_bank = ps("eT_bank")
        mix_bank = ps("mix_bank")
        w3_bank = eT_bank
        xT_bank, x2T_bank = score_bank
        y_bank = mix_bank

        x_loaded = sem("x_loaded")
        x_res_loaded = sem("x_res_loaded")
        w_loaded = [sem(f"w_loaded{c}") for c in range(len(WEIGHT_PARTS))]
        columns_loaded = sem("columns_loaded")
        out_stored = sem("out_stored")
        x1_saved, x1_tail_loaded = sem("x1_saved"), sem("x1_tail_loaded")
        consts_zeroed = sem("consts_zeroed")
        consts_ready = sem("consts_ready")
        w_hi_ready, w_lo_ready = sem("w_hi_ready"), sem("w_lo_ready")
        lo_summed, lo_gathered, lo_known = sem("lo_summed"), sem("lo_gathered"), sem("lo_known")
        neg_wlr_ready = sem("neg_wlr_ready")
        xT_turned, x2T_turned, y_turned = sem("xT_turned"), sem("x2T_turned"), sem("y_turned")
        scores_done, eT_turned, pv_done = sem("scores_done"), sem("eT_turned"), sem("pv_done")
        gated_mm, h1_mm, h2_mm = sem("gated_mm"), sem("h1_mm"), sem("h2_mm")
        w3_mm = sem("w3_mm")
        xT_hi_ready = sem("xT_hi_ready")
        exp_done, eT_hi_ready = sem("exp_done"), sem("eT_hi_ready")
        gate_ready, gelu1_done, gelu2_done = sem("gate_ready"), sem("gelu1_done"), sem("gelu2_done")
        yT_ready, x2T_hi_ready = sem("yT_ready"), sem("x2T_hi_ready")
        max_ready, eT_lo_ready = sem("max_ready"), sem("eT_lo_ready")
        gated_done = sem("gated_done")
        hA_lo_ready, hB_lo_ready, hC_lo_ready = (sem(f"h{c}_lo_ready") for c in "ABC")
        xT_lo_ready = sem("xT_lo_ready")
        x2T_lo_ready, xn_lo_ready = sem("x2T_lo_ready"), sem("xn_lo_ready")
        x1_ready, y_ready = sem("x1_ready"), sem("y_ready")
        hA_hi_ready = sem("hA_hi_ready")
        xn_ready, xn_hi_ready, x2n_ready = sem("xn_ready"), sem("xn_hi_ready"), sem("x2n_ready")
        att_base_ready, ffn_base_ready = sem("att_base_ready"), sem("ffn_base_ready")
        rs_chain = sem("rs_chain")

        waits_apart = sem("waits_apart")

        class Norm:
            def __init__(self, name):
                self.stats = sb(f"{name}_stats", [P, T, 6], f32)
                self.mean_var = sb(f"{name}_mean_var", [P, T, 2], f32)
                self.var_eps = sb(f"{name}_var_eps", [P, T], f32)
                self.rstd = sb(f"{name}_rstd", [P, T], f32)
                self.scaled_mean = sb(f"{name}_scaled_mean", [P, T], f32)
                self.shift = sb(f"{name}_shift", [P, T], f32)
                self.stats_done = sem(f"{name}_stats_done")
                self.mean_var_done = sem(f"{name}_mean_var_done")
                self.chain = sem(f"{name}_chain")

        ln_x, ln_att, ln_x1, ln_y = Norm("ln_x"), Norm("ln_att"), Norm("ln_x1"), Norm("ln_y")
        rs_squared = sb("rs_squared", [P, T], f32)
        rs_eps = sb("rs_eps", [P, T], f32)

        def apart(eng):
            eng.sem_inc(waits_apart, 1)

        def wait_free(eng, semaphore, per, b, count):
            if isinstance(b, int):
                if per * b + count > 0:
                    eng.wait_ge(semaphore, min(per * b + count, per * N))
            else:
                eng.wait_ge(semaphore, b * per + count)

        def x_view(dram, b):
            return dram[b, :, :].rearrange("(p t) d -> p t d", t=T)

        block = ctx.enter_context(nc.Block())

        class Stages:
            def __init__(self, i, full=False):
                def batch(b):
                    return b if full or 0 <= b < N else None
                self.prep, self.att, self.mid, self.ffn, self.tail = (batch(i + d) for d in (1, 0, -1, -2, -3))

        def steps(eng, step):
            for i in (2, 3):
                step(Stages(i))
            with eng.Fori(4, N - 1) as i:
                step(Stages(i, full=True))
            step(Stages(N - 1))

        @block.sync
        def _(sp):
            def load_x(b):
                wait_free(sp, xn_ready, 1, b, 0)
                sp.dma_start(x_in[:, :, :], x_view(x_dram, b)).then_inc(x_loaded, 16)

            def load_x_res(a):
                wait_free(sp, att_base_ready, 1, a, 0)
                sp.dma_start(x_res[:, :, :], x_view(x_dram, a)).then_inc(x_res_loaded, 16)

            def save_x1(b):
                sp.wait_ge(x1_ready, b + 1)
                sp.dma_start(x1_all[:, b, :], x1[:, :, :].rearrange("p t d -> p (t d)")).then_inc(x1_saved, 16)

            def load_x1_tail(g):
                sp.wait_ge(x1_saved, g * 16 + 16)
                wait_free(sp, ffn_base_ready, 1, g, 0)
                sp.dma_start(x1_tail[:, :, :].rearrange("p t d -> p (t d)"), x1_all[:, g, :]).then_inc(x1_tail_loaded, 16)

            def store(g):
                sp.wait_ge(y_ready, g + 1)
                sp.dma_start(x_view(out_dram, g), y_out[:, :, :]).then_inc(out_stored, 16)

            def step(st):
                a, b, g = st.att, st.mid, st.tail
                if st.prep is not None:
                    load_x(st.prep)
                if g is not None:
                    load_x1_tail(g)
                    store(g)
                if b is not None:
                    save_x1(b)
                if a is not None:
                    load_x_res(a)

            def start():
                load_x_res(0)
                load_x(1)
                load_x(2)
                load_x_res(1)
                save_x1(0)

            def finish():
                load_x1_tail(N - 3)
                store(N - 3)
                load_x1_tail(N - 2)
                store(N - 2)
                save_x1(N - 1)
                load_x1_tail(N - 1)
                store(N - 1)

            def load_weights(c):
                part = WEIGHT_PARTS[c]
                sp.dma_start(w_raw[:, part], weights_dram[:, part]).then_inc(w_loaded[c], 16)

            load_x(0)
            sp.dma_start(columns[:, :], columns_dram).then_inc(columns_loaded, 16)
            for c in range(len(WEIGHT_PARTS)):
                load_weights(c)
            start()
            steps(sp, step)
            finish()
            sp.wait_ge(out_stored, 16 * N)

        @block.tensor
        def _(pe):
            def matmuls(out, pairs):
                for n, (lhs, rhs) in enumerate(pairs):
                    mm = nc.tensor.matmul(out, lhs, rhs, start=(n == 0), stop=(n == len(pairs) - 1))
                return mm

            def turn(bank, src, done):
                for t in range(T):
                    mm = nc.tensor.transpose(bank[:, t * P:(t + 1) * P], src[:, t * P:(t + 1) * P], ident[:, :])
                mm.then_inc(done, 1)

            def turn_x(b):
                pe.wait_ge(xn_ready, b + 1)
                wait_free(pe, exp_done, T, b, -1)
                turn(xT_bank, xn[:, :, :].rearrange("p t d -> p (t d)"), xT_turned)

            def scores(b, j):
                if j == 0:
                    pe.wait_ge(xT_lo_ready, b * 2 + 2)
                if j == 1:
                    wait_free(pe, x2T_lo_ready, 1, b, -1)
                wait_free(pe, exp_done, T, b, j - 1)
                rows = slice(j * P, (j + 1) * P)
                matmuls(score_bank[j % 2][:, :], [
                    (aT_hi[:, rows], xT_hi[:, :]), (aT_hi[:, rows], xT_lo[:, :]), (aT_lo[:, rows], xT_hi[:, :]),
                ]).then_inc(scores_done, 1)

            def turn_e(b, j):
                pe.wait_ge(exp_done, b * T + j + 1)
                if j == 0:
                    wait_free(pe, yT_ready, 1, b, -2)
                wait_free(pe, eT_lo_ready, T, b, j)
                turn(eT_bank, exps[:, j, :], eT_turned)

            def attend(b, j):
                if j == 0:
                    pe.wait_ge(xn_lo_ready, b + 1)
                    wait_free(pe, y_ready, 1, b, -2)
                    wait_free(pe, x1_ready, 1, b, 0)
                pe.wait_ge(eT_lo_ready, b * T + j + 1)
                pairs = []
                for t in range(T):
                    hi, lo = eT_hi[:, j, t, :], eT_lo[:, j, t, :]
                    pairs += [(hi, xn_hi[:, t, :]), (hi, xn_lo[:, t, :]), (lo, xn_hi[:, t, :])]
                matmuls(mix_bank[:, j * P:(j + 1) * P], pairs).then_inc(pv_done, 1)

            def turn_x2(b):
                pe.wait_ge(x2n_ready, b + 1)
                wait_free(pe, exp_done, T, b, 2 * T)
                wait_free(pe, x2T_lo_ready, 1, b, 0)
                turn(x2T_bank, x2n[:, :, :].rearrange("p t d -> p (t d)"), x2T_turned)

            def products(general, col, hi, lo):
                w = slice(col, col + P)
                pairs = [(w_hi[:, w], hi), (w_hi[:, w], lo)]
                return pairs + ([(w_lo[:, w], hi)] if general else [])

            def gated(general, b, m):
                if m == 0:
                    pe.wait_ge(x2T_lo_ready, b + 1)
                if m < 2:
                    wait_free(pe, gelu2_done, K, b, 2 * m + 2 - K)
                else:
                    wait_free(pe, gated_done, K, b, m - 1)
                for bank, w in ((hid_bank[2 * (m % 2)], W1), (hid_bank[2 * (m % 2) + 1], W2)):
                    mm = matmuls(bank[:, :], products(general, w + m * P, x2T_hi[:, :], x2T_lo[:, :]))
                mm.then_inc(gated_mm, 1)

            def hidden(general, b, tiles, ks, w, hi, lo, lo_ready, bank_read, tiles_read, done):
                for m in tiles:
                    if 0 in ks:
                        pe.wait_ge(bank_read, b * K + tiles_read(m))
                    for k in ks:
                        if m == 0:
                            pe.wait_ge(lo_ready, b * K + k + 1)
                        pairs = products(general, w + k * H + m * P, hi[:, k, :], lo[:, k, :])
                        for n, (lhs, rhs) in enumerate(pairs):
                            mm = nc.tensor.matmul(hid_bank[m][:, :], lhs, rhs, start=(k == 0 and n == 0),
                                                  stop=(k == K - 1 and n == len(pairs) - 1))
                    if K - 1 in ks:
                        mm.then_inc(done, 1)

            def layer1(general, b, tiles, ks):
                hidden(general, b, tiles, ks, H1, hA_hi, hA_lo, hA_lo_ready,
                       gated_done, lambda m: 3 + m // 2, h1_mm)

            def layer2(general, b, tiles, ks):
                hidden(general, b, tiles, ks, H2, hB_hi, hB_lo, hB_lo_ready,
                       gelu1_done, lambda m: m + 1, h2_mm)

            def layer3(general, b, ks):
                if 0 in ks:
                    wait_free(pe, eT_lo_ready, T, b, 3 * T)
                    wait_free(pe, yT_ready, 1, b, 0)
                for k in ks:
                    pe.wait_ge(hC_lo_ready, b * K + k + 1)
                    pairs = products(general, W3 + k * P, hC_hi[:, k, :], hC_lo[:, k, :])
                    for n, (lhs, rhs) in enumerate(pairs):
                        mm = nc.tensor.matmul(w3_bank[:, :], lhs, rhs, start=(k == 0 and n == 0),
                                              stop=(k == K - 1 and n == len(pairs) - 1))
                if K - 1 in ks:
                    mm.then_inc(w3_mm, 1)

            def turn_y(b):
                pe.wait_ge(yT_ready, b + 1)
                wait_free(pe, x1_ready, 1, b, 3)
                wait_free(pe, y_ready, 1, b, 0)
                turn(y_bank, yT, y_turned)

            def gather_lo():
                pe.wait_ge(lo_summed, len(WEIGHT_PARTS))
                nc.tensor.matmul(hid_bank[0][:, 0:len(WEIGHT_PARTS)], ones[:, :], lo_sum[:, :], start=True,
                                 stop=True).then_inc(lo_gathered, 1)

            def start():
                turn_x(0)
                scores(0, 0)
                scores(0, 1)
                turn_e(0, 0)
                scores(0, 2)
                scores(0, 3)
                turn_e(0, 1)
                turn_e(0, 2)
                turn_x(1)
                attend(0, 0)
                turn_e(0, 3)
                attend(0, 1)
                attend(0, 2)
                attend(0, 3)
                scores(1, 0)
                scores(1, 1)
                turn_e(1, 0)
                scores(1, 2)
                scores(1, 3)
                turn_e(1, 1)
                attend(1, 0)
                turn_e(1, 2)
                turn_x(2)
                attend(1, 1)
                turn_e(1, 3)
                turn_x2(0)
                gather_lo()
                attend(1, 2)
                attend(1, 3)

            def main(general):
                def step(st):
                    a, f, g = st.att, st.ffn, st.tail
                    if f is not None:
                        gated(general, f, 0)
                    if g is not None:
                        layer3(general, g, (0,))
                    if f is not None:
                        gated(general, f, 1)
                    if a is not None:
                        scores(a, 0)
                    if f is not None:
                        gated(general, f, 2)
                    if g is not None:
                        layer3(general, g, (1,))
                    if f is not None:
                        gated(general, f, 3)
                    if g is not None:
                        layer3(general, g, (2,))
                    if a is not None:
                        scores(a, 1)
                    if f is not None:
                        layer1(general, f, (0,), (0,))
                    if g is not None:
                        layer3(general, g, (3,))
                    if f is not None:
                        layer1(general, f, (1, 2, 3), (0,))
                    if a is not None:
                        scores(a, 2)
                    if f is not None:
                        layer1(general, f, (0,), (1,))
                    if a is not None:
                        scores(a, 3)
                        turn_e(a, 0)
                    if f is not None:
                        layer1(general, f, (1, 2), (1,))
                        layer1(general, f, (0,), (2,))
                        layer1(general, f, (3,), (1,))
                        layer1(general, f, (1,), (2,))
                        layer1(general, f, (0,), (3,))
                        layer1(general, f, (2,), (2,))
                    if g is not None:
                        turn_y(g)
                    if f is not None:
                        layer1(general, f, (1,), (3,))
                        layer1(general, f, (3,), (2,))
                        layer1(general, f, (2,), (3,))
                    if a is not None:
                        turn_e(a, 1)
                    if f is not None:
                        layer1(general, f, (3,), (3,))
                        layer2(general, f, (0,), (0,))
                    if st.prep is not None:
                        turn_x(st.prep)
                    if f is not None:
                        layer2(general, f, (1,), (0,))
                        layer2(general, f, (0,), (1,))
                        layer2(general, f, (2,), (0,))
                        layer2(general, f, (1,), (1,))
                        layer2(general, f, (0,), (2,))
                        layer2(general, f, (2,), (1,))
                        layer2(general, f, (3,), (0,))
                    if a is not None:
                        turn_e(a, 2)
                    if f is not None:
                        layer2(general, f, (3,), (1,))
                        layer2(general, f, (0,), (3,))
                        layer2(general, f, (1, 2), (2,))
                        layer2(general, f, (1,), (3,))
                        layer2(general, f, (3,), (2,))
                        layer2(general, f, (2,), (3,))
                    if a is not None:
                        attend(a, 0)
                        turn_e(a, 3)
                    if st.mid is not None:
                        turn_x2(st.mid)
                    if a is not None:
                        attend(a, 1)
                    if f is not None:
                        layer2(general, f, (3,), (3,))
                    if a is not None:
                        attend(a, 2)
                        attend(a, 3)

                def finish():
                    gated(general, N - 2, 0)
                    gated(general, N - 2, 1)
                    layer3(general, N - 3, (0, 1))
                    gated(general, N - 2, 2)
                    gated(general, N - 2, 3)
                    layer3(general, N - 3, (2, 3))
                    layer1(general, N - 2, (0,), (0, 1))
                    layer1(general, N - 2, (1, 3), (0,))
                    layer1(general, N - 2, (1, 3), (1,))
                    layer1(general, N - 2, (0,), (2,))
                    layer1(general, N - 2, (2,), (0,))
                    layer1(general, N - 2, (0,), (3,))
                    layer1(general, N - 2, (1,), (2,))
                    layer1(general, N - 2, (2,), (1,))
                    layer1(general, N - 2, (1,), (3,))
                    layer1(general, N - 2, (2,), (2, 3))
                    layer1(general, N - 2, (3,), (2,))
                    layer2(general, N - 2, (0,), (0,))
                    layer1(general, N - 2, (3,), (3,))
                    layer2(general, N - 2, (1,), (0,))
                    layer2(general, N - 2, (0,), (1,))
                    turn_y(N - 3)
                    layer2(general, N - 2, (1,), (1,))
                    layer2(general, N - 2, (0,), (2,))
                    layer2(general, N - 2, (2,), (0,))
                    layer2(general, N - 2, (0,), (3,))
                    layer2(general, N - 2, (1,), (2,))
                    layer2(general, N - 2, (2,), (1,))
                    turn_x2(N - 1)
                    layer2(general, N - 2, (1,), (3,))
                    layer2(general, N - 2, (2,), (2,))
                    layer2(general, N - 2, (3,), (0,))
                    layer2(general, N - 2, (2,), (3,))
                    layer2(general, N - 2, (3,), (1, 2, 3))
                    gated(general, N - 1, 0)
                    gated(general, N - 1, 1)
                    layer3(general, N - 2, (0, 1, 2, 3))
                    gated(general, N - 1, 2)
                    gated(general, N - 1, 3)
                    turn_y(N - 2)
                    layer1(general, N - 1, (0, 1), (0,))
                    layer1(general, N - 1, (0,), (1,))
                    layer1(general, N - 1, (2,), (0, 1))
                    layer1(general, N - 1, (3,), (0,))
                    layer1(general, N - 1, (0,), (2,))
                    layer1(general, N - 1, (1,), (1,))
                    layer1(general, N - 1, (0,), (3,))
                    layer1(general, N - 1, (1,), (2,))
                    layer1(general, N - 1, (3,), (1,))
                    layer1(general, N - 1, (1,), (3,))
                    layer1(general, N - 1, (2, 3), (2,))
                    layer1(general, N - 1, (2,), (3,))
                    layer2(general, N - 1, (0,), (0,))
                    layer1(general, N - 1, (3,), (3,))
                    layer2(general, N - 1, (1,), (0,))
                    layer2(general, N - 1, (0,), (1,))
                    layer2(general, N - 1, (2,), (0, 1))
                    layer2(general, N - 1, (0,), (2,))
                    layer2(general, N - 1, (1,), (1,))
                    layer2(general, N - 1, (0,), (3,))
                    layer2(general, N - 1, (1,), (2, 3))
                    layer2(general, N - 1, (2,), (2,))
                    layer2(general, N - 1, (3,), (0,))
                    layer2(general, N - 1, (2,), (3,))
                    layer2(general, N - 1, (3,), (1, 2, 3))
                    layer3(general, N - 1, (0, 1, 2, 3))
                    turn_y(N - 1)

                steps(pe, step)
                finish()

            pe.wait_ge(consts_ready, 2)
            start()
            pe.wait_ge(lo_known, 1)
            any_lo = pe.value_load(lo_total[0:1, 0:1].bitcast(i32))
            with pe.If(any_lo != 0):
                main(general=True)
            with pe.Else():
                main(general=False)

        @block.scalar
        def _(act):
            def high_xT(b):
                act.wait_ge(xT_turned, b + 1)
                wait_free(act, scores_done, T, b, 0)
                nc.scalar.copy(xT_hi[:, :], xT_bank[:, :]).then_inc(xT_hi_ready, 1)

            def high_aT(b):
                nc.scalar.mul(aT_hi[:, :], xT_bank[:, :], neg_wlr[:, 0:1]).then_inc(xT_hi_ready, 1)

            def softmax(b, j):
                act.wait_ge(max_ready, b * T + j + 1)
                wait_free(act, eT_turned, T, b, j + 1 - T)
                if j == 0:
                    wait_free(act, rs_chain, 2, b, -1)
                nc.scalar.activation(exps[:, j, :], score_bank[j % 2][:, :], ACT.Exp, bias=neg_max[:, j:j + 1],
                                     scale=-1.0, accum_out=row_sum[:, j:j + 1]).then_inc(exp_done, 1)

            def high_e(b, j):
                act.wait_ge(eT_turned, b * T + j + 1)
                wait_free(act, pv_done, T, b, j + 1 - T)
                nc.scalar.copy(eT_hi[:, j, :, :].rearrange("p t s -> p (t s)"), eT_bank[:, :]).then_inc(eT_hi_ready, 1)

            def silu(b, m):
                if m == 0:
                    nc.scalar.activation(table_loader[:, :], columns[:, 0:1], ACT.Silu)
                act.wait_ge(gated_mm, b * K + m + 1)
                wait_free(act, gated_done, K, b, m - 1)
                nc.scalar.activation(gate[:, m % 2, :], hid_bank[2 * (m % 2)][:, :], ACT.Silu,
                                     scale=columns[:, S1 + m:S1 + m + 1]).then_inc(gate_ready, 1)

            def gelu(b, m, mm, col, last_lo, hi, hi_used, per, count, done):
                act.wait_ge(mm, b * K + m + 1)
                act.wait_ge(last_lo, b * K + m + 1)
                if m == 0:
                    wait_free(act, hi_used, per, b, count)
                scale = columns[:, col + m:col + m + 1]
                nc.scalar.activation(h_full[:, m, :], hid_bank[m][:, :], ACT.Gelu, scale=scale)
                nc.scalar.activation(hi[:, m, :], hid_bank[m][:, :], ACT.Gelu, scale=scale).then_inc(done, 1)

            def gelu1(b, m):
                gelu(b, m, h1_mm, SH1, hA_lo_ready, hB_hi, h2_mm, K, 0, gelu1_done)

            def gelu2(b, m):
                gelu(b, m, h2_mm, SH2, hB_lo_ready, hC_hi, w3_mm, 1, 0, gelu2_done)

            def scale_y(b):
                act.wait_ge(w3_mm, b + 1)
                wait_free(act, y_turned, 1, b, 0)
                nc.scalar.mul(yT[:, :], w3_bank[:, :], columns[:, S3:S3 + 1]).then_inc(yT_ready, 1)

            def high_x2T(b):
                act.wait_ge(x2T_turned, b + 1)
                wait_free(act, gated_mm, K, b, 0)
                nc.scalar.copy(x2T_hi[:, :], x2T_bank[:, :]).then_inc(x2T_hi_ready, 1)

            def high_weights(c):
                part = WEIGHT_PARTS[c]
                act.wait_ge(w_loaded[c], 16)
                nc.scalar.copy(w_hi[:, part], w_raw[:, part]).then_inc(w_hi_ready, 1)

            def sum_lo(c):
                part = WEIGHT_PARTS[c]
                act.wait_ge(w_lo_ready, c + 1)
                nc.scalar.activation(w_raw[:, part], w_lo[:, part].bitcast(f32), ACT.Abs,
                                     accum_out=lo_sum[:, c:c + 1]).then_inc(lo_summed, 1)

            def step(st):
                a, b, f, g = st.att, st.mid, st.ffn, st.tail
                if f is not None:
                    silu(f, 0)
                    silu(f, 1)
                    silu(f, 2)
                    silu(f, 3)
                if a is not None:
                    softmax(a, 0)
                    softmax(a, 1)
                if g is not None:
                    scale_y(g)
                if a is not None:
                    softmax(a, 2)
                    high_e(a, 0)
                    softmax(a, 3)
                if f is not None:
                    gelu1(f, 0)
                    gelu1(f, 1)
                    gelu1(f, 2)
                if a is not None:
                    high_e(a, 1)
                if f is not None:
                    gelu1(f, 3)
                if st.prep is not None:
                    high_xT(st.prep)
                    high_aT(st.prep)
                if a is not None:
                    high_e(a, 2)
                if f is not None:
                    gelu2(f, 0)
                    gelu2(f, 1)
                    gelu2(f, 2)
                if a is not None:
                    high_e(a, 3)
                if b is not None:
                    high_x2T(b)
                if f is not None:
                    gelu2(f, 3)

            def start():
                high_weights(0)
                high_weights(1)
                sum_lo(0)
                high_xT(0)
                high_aT(0)
                high_weights(2)
                high_weights(3)
                softmax(0, 0)
                softmax(0, 1)
                high_e(0, 0)
                high_e(0, 1)
                softmax(0, 2)
                softmax(0, 3)
                high_e(0, 2)
                high_xT(1)
                high_aT(1)
                high_e(0, 3)
                high_weights(4)
                high_weights(5)
                sum_lo(1)
                sum_lo(2)
                sum_lo(3)
                sum_lo(4)
                sum_lo(5)
                softmax(1, 0)
                softmax(1, 1)
                high_e(1, 0)
                high_e(1, 1)
                softmax(1, 2)
                softmax(1, 3)
                high_e(1, 2)
                high_xT(2)
                high_aT(2)
                high_e(1, 3)
                high_x2T(0)

            def finish():
                silu(N - 2, 0)
                silu(N - 2, 1)
                silu(N - 2, 2)
                silu(N - 2, 3)
                scale_y(N - 3)
                gelu1(N - 2, 0)
                gelu1(N - 2, 1)
                gelu1(N - 2, 2)
                gelu1(N - 2, 3)
                gelu2(N - 2, 0)
                high_x2T(N - 1)
                gelu2(N - 2, 1)
                gelu2(N - 2, 2)
                gelu2(N - 2, 3)
                silu(N - 1, 0)
                silu(N - 1, 1)
                scale_y(N - 2)
                silu(N - 1, 2)
                silu(N - 1, 3)
                gelu1(N - 1, 0)
                gelu1(N - 1, 1)
                gelu1(N - 1, 2)
                gelu1(N - 1, 3)
                gelu2(N - 1, 0)
                gelu2(N - 1, 1)
                gelu2(N - 1, 2)
                gelu2(N - 1, 3)
                scale_y(N - 1)

            act.wait_ge(columns_loaded, 16)
            act.wait_ge(neg_wlr_ready, 1)
            start()
            steps(act, step)
            finish()

        @block.vector
        def _(dve):
            def minus(out, a, b):
                return nc.vector.tensor_tensor(out, a, b, ALU.subtract)

            def statistics(norm, tile):
                for t in range(T):
                    op = nc.vector.bn_stats(norm.stats[:, t, :], tile(t))
                op.then_inc(norm.stats_done, 1)

            def aggregate(norm, b):
                dve.wait_ge(norm.stats_done, b + 1)
                apart(dve)
                for t in range(T):
                    op = nc.vector.bn_aggr(norm.mean_var[:, t, :], norm.stats[:, t, :])
                op.then_inc(norm.mean_var_done, 1)

            def row_max(b, j):
                dve.wait_ge(scores_done, b * T + j + 1)
                nc.vector.tensor_reduce(neg_max[:, j:j + 1], score_bank[j % 2][:, :], AX.X, ALU.min).then_inc(max_ready, 1)

            def low_e(b, j):
                dve.wait_ge(eT_hi_ready, b * T + j + 1)
                minus(eT_lo[:, j, :, :].rearrange("p t s -> p (t s)"), eT_bank[:, :],
                      eT_hi[:, j, :, :].rearrange("p t s -> p (t s)")).then_inc(eT_lo_ready, 1)

            def gated(b, m):
                wait_free(dve, hC_lo_ready, K, b, m + 1 - K)
                dve.wait_ge(gate_ready, b * K + m + 1)
                nc.vector.scalar_tensor_tensor(h_full[:, m, :], hid_bank[2 * (m % 2) + 1][:, :],
                                               columns[:, S2 + m:S2 + m + 1], gate[:, m % 2, :],
                                               ALU.mult, ALU.mult).then_inc(gated_done, 1)

            def high_A(b, m):
                if m == 0:
                    wait_free(dve, h1_mm, K, b, 0)
                dve.wait_ge(gated_done, b * K + m + 1)
                nc.vector.tensor_copy(hA_hi[:, m, :], h_full[:, m, :]).then_inc(hA_hi_ready, 1)

            def split_h(b, m, hi_ready, hi, lo, lo_ready):
                dve.wait_ge(hi_ready, b * K + m + 1)
                minus(lo[:, m, :], h_full[:, m, :], hi[:, m, :].bitcast(f32)).then_inc(lo_ready, 1)

            def low_A(b, m):
                split_h(b, m, hA_hi_ready, hA_hi, hA_lo, hA_lo_ready)

            def low_B(b, m):
                split_h(b, m, gelu1_done, hB_hi, hB_lo, hB_lo_ready)

            def low_C(b, m):
                split_h(b, m, gelu2_done, hC_hi, hC_lo, hC_lo_ready)

            def x_statistics(b):
                dve.wait_ge(x_loaded, b * 16 + 16)
                statistics(ln_x, lambda t: x_in[:, t, :])

            def low_xn(b):
                dve.wait_ge(xn_hi_ready, b + 1)
                minus(xn_lo[:, :, :], xn[:, :, :], xn_hi[:, :, :]).then_inc(xn_lo_ready, 1)

            def low_xT(b):
                dve.wait_ge(xT_hi_ready, b * 2 + 2)
                minus(xT_lo[:, :], xT_bank[:, :], xT_hi[:, :].bitcast(f32)).then_inc(xT_lo_ready, 1)

            def low_aT(b):
                dve.wait_ge(xT_hi_ready, b * 2 + 2)
                nc.vector.scalar_tensor_tensor(aT_lo[:, :], xT_bank[:, :], neg_wlr[:, 0:1], aT_hi[:, :].bitcast(f32),
                                               ALU.mult, ALU.subtract).then_inc(xT_lo_ready, 1)

            def scaled_add(norm, b, src, base, base_ready, out, done):
                dve.wait_ge(base_ready, b + 1)
                for t in range(T):
                    op = nc.vector.scalar_tensor_tensor(out[:, t, :], src[:, t * P:(t + 1) * P], norm.rstd[:, t:t + 1],
                                                        base[:, t, :], ALU.mult, ALU.add)
                op.then_inc(done, 1)

            def add_attention(b):
                wait_free(dve, x1_saved, 16, b, 0)
                wait_free(dve, x2n_ready, 1, b, 0)
                scaled_add(ln_att, b, mix_bank, att_base, att_base_ready, x1, x1_ready)

            def x1_statistics(b):
                dve.wait_ge(x1_ready, b + 1)
                statistics(ln_x1, lambda t: x1[:, t, :])

            def low_x2T(b):
                dve.wait_ge(x2T_hi_ready, b + 1)
                minus(x2T_lo[:, :], x2T_bank[:, :], x2T_hi[:, :].bitcast(f32)).then_inc(x2T_lo_ready, 1)

            def y_statistics(b):
                dve.wait_ge(y_turned, b + 1)
                statistics(ln_y, lambda t: y_bank[:, t * P:(t + 1) * P])

            def add_ffn(b):
                wait_free(dve, out_stored, 16, b, 0)
                scaled_add(ln_y, b, y_bank, ffn_base, ffn_base_ready, y_out, y_ready)

            def attention_statistics(b):
                dve.wait_ge(pv_done, b * T + T)
                statistics(ln_att, lambda t: mix_bank[:, t * P:(t + 1) * P])

            def low_weights(c):
                part = WEIGHT_PARTS[c]
                dve.wait_ge(w_hi_ready, c + 1)
                minus(w_lo[:, part], w_raw[:, part], w_hi[:, part].bitcast(f32)).then_inc(w_lo_ready, 1)

            def total_lo():
                dve.wait_ge(lo_gathered, 1)
                nc.vector.tensor_reduce(lo_total[:, :], hid_bank[0][:, 0:len(WEIGHT_PARTS)], AX.X, ALU.add).then_inc(lo_known, 1)

            def step(st):
                a, b, f, g = st.att, st.mid, st.ffn, st.tail
                if f is not None:
                    gated(f, 0)
                    high_A(f, 0)
                    gated(f, 1)
                    low_A(f, 0)
                    high_A(f, 1)
                    gated(f, 2)
                if a is not None:
                    row_max(a, 0)
                if f is not None:
                    high_A(f, 2)
                    gated(f, 3)
                    low_A(f, 1)
                if a is not None:
                    row_max(a, 1)
                if st.prep is not None:
                    x_statistics(st.prep)
                if a is not None:
                    row_max(a, 2)
                if f is not None:
                    low_A(f, 2)
                    high_A(f, 3)
                if a is not None:
                    row_max(a, 3)
                if st.prep is not None:
                    aggregate(ln_x, st.prep)
                if f is not None:
                    low_A(f, 3)
                if b is not None:
                    add_attention(b)
                if a is not None:
                    low_xn(a)
                    low_e(a, 0)
                if g is not None:
                    y_statistics(g)
                if f is not None:
                    low_B(f, 0)
                if g is not None:
                    aggregate(ln_y, g)
                if f is not None:
                    low_B(f, 1)
                    low_B(f, 2)
                if b is not None:
                    x1_statistics(b)
                if a is not None:
                    low_e(a, 1)
                if b is not None:
                    aggregate(ln_x1, b)
                if f is not None:
                    low_B(f, 3)
                if st.prep is not None:
                    low_xT(st.prep)
                    low_aT(st.prep)
                if g is not None:
                    add_ffn(g)
                if a is not None:
                    low_e(a, 2)
                if f is not None:
                    low_C(f, 0)
                    low_C(f, 1)
                    low_C(f, 2)
                if a is not None:
                    low_e(a, 3)
                if b is not None:
                    low_x2T(b)
                if a is not None:
                    attention_statistics(a)
                if f is not None:
                    low_C(f, 3)
                if a is not None:
                    aggregate(ln_att, a)

            def start():
                x_statistics(0)
                aggregate(ln_x, 0)
                low_weights(0)
                low_weights(1)
                low_xT(0)
                low_aT(0)
                x_statistics(1)
                row_max(0, 0)
                aggregate(ln_x, 1)
                row_max(0, 1)
                low_weights(2)
                low_xn(0)
                low_e(0, 0)
                row_max(0, 2)
                row_max(0, 3)
                low_e(0, 1)
                low_weights(3)
                low_e(0, 2)
                x_statistics(2)
                low_xT(1)
                low_e(0, 3)
                aggregate(ln_x, 2)
                low_aT(1)
                attention_statistics(0)
                aggregate(ln_att, 0)
                low_weights(4)
                low_weights(5)
                low_xn(1)
                row_max(1, 0)
                row_max(1, 1)
                add_attention(0)
                x1_statistics(0)
                low_e(1, 0)
                row_max(1, 2)
                aggregate(ln_x1, 0)
                row_max(1, 3)
                low_e(1, 1)
                low_e(1, 2)
                low_xT(2)
                low_e(1, 3)
                total_lo()
                low_x2T(0)
                low_aT(2)
                attention_statistics(1)
                aggregate(ln_att, 1)

            def finish():
                gated(N - 2, 0)
                high_A(N - 2, 0)
                gated(N - 2, 1)
                low_A(N - 2, 0)
                high_A(N - 2, 1)
                gated(N - 2, 2)
                low_A(N - 2, 1)
                gated(N - 2, 3)
                high_A(N - 2, 2)
                high_A(N - 2, 3)
                low_A(N - 2, 2)
                low_A(N - 2, 3)
                add_attention(N - 1)
                x1_statistics(N - 1)
                aggregate(ln_x1, N - 1)
                low_B(N - 2, 0)
                low_B(N - 2, 1)
                low_B(N - 2, 2)
                low_B(N - 2, 3)
                y_statistics(N - 3)
                aggregate(ln_y, N - 3)
                low_x2T(N - 1)
                low_C(N - 2, 0)
                low_C(N - 2, 1)
                low_C(N - 2, 2)
                low_C(N - 2, 3)
                add_ffn(N - 3)
                gated(N - 1, 0)
                high_A(N - 1, 0)
                gated(N - 1, 1)
                low_A(N - 1, 0)
                high_A(N - 1, 1)
                gated(N - 1, 2)
                low_A(N - 1, 1)
                gated(N - 1, 3)
                high_A(N - 1, 2)
                high_A(N - 1, 3)
                low_A(N - 1, 2)
                low_A(N - 1, 3)
                y_statistics(N - 2)
                aggregate(ln_y, N - 2)
                low_B(N - 1, 0)
                low_B(N - 1, 1)
                low_B(N - 1, 2)
                low_B(N - 1, 3)
                add_ffn(N - 2)
                low_C(N - 1, 0)
                low_C(N - 1, 1)
                low_C(N - 1, 2)
                low_C(N - 1, 3)
                y_statistics(N - 1)
                aggregate(ln_y, N - 1)
                add_ffn(N - 1)

            dve.wait_ge(columns_loaded, 16)
            nc.vector.scalar_tensor_tensor(neg_wlr[:, :], columns[:, WL:WL + 1], -1.0, columns[:, WR:WR + 1],
                                           ALU.mult, ALU.mult).then_inc(neg_wlr_ready, 1)
            dve.wait_ge(neg_wlr_ready, 1)
            start()
            steps(dve, step)
            finish()

        @block.gpsimd
        def _(pool):
            def rstd(norm, b, eps=None):
                mean, var = norm.mean_var[:, :, 0], norm.mean_var[:, :, 1]
                pool.wait_ge(norm.mean_var_done, b + 1)
                apart(pool)
                if eps is None:
                    nc.gpsimd.tensor_scalar(norm.var_eps[:, :], var, EPS, 1.0, ALU.add, ALU.mult).then_inc(norm.chain, 1)
                else:
                    nc.gpsimd.tensor_tensor(norm.var_eps[:, :], var, eps, ALU.add).then_inc(norm.chain, 1)
                pool.wait_ge(norm.chain, b * 4 + 1)
                nc.gpsimd.tensor_tensor(norm.rstd[:, :], norm.var_eps[:, :], minus_half[:, :], ALU.pow).then_inc(norm.chain, 1)
                pool.wait_ge(norm.chain, b * 4 + 2)
                nc.gpsimd.tensor_tensor(norm.scaled_mean[:, :], mean, norm.rstd[:, :], ALU.mult).then_inc(norm.chain, 1)
                pool.wait_ge(norm.chain, b * 4 + 3)
                apart(pool)
                nc.gpsimd.tensor_scalar(norm.shift[:, :], norm.scaled_mean[:, :], -1.0, 1.0, ALU.mult, ALU.mult).then_inc(norm.chain, 1)
                pool.wait_ge(norm.chain, b * 4 + 4)
                apart(pool)

            def shifted(norm, src, out, done):
                for t in range(T):
                    op = nc.gpsimd.tensor_scalar(out[:, t, :], src[:, t, :], 1.0, norm.shift[:, t:t + 1], ALU.mult, ALU.add)
                op.then_inc(done, 1)

            def normalized(norm, src, out, done):
                for t in range(T):
                    op = nc.gpsimd.tensor_scalar(out[:, t, :], src[:, t, :], norm.rstd[:, t:t + 1],
                                                 norm.shift[:, t:t + 1], ALU.mult, ALU.add)
                op.then_inc(done, 1)

            def normalize_x(b):
                wait_free(pool, xT_turned, 1, b, 0)
                wait_free(pool, xn_lo_ready, 1, b, 0)
                apart(pool)
                normalized(ln_x, x_in, xn, xn_ready)

            def high_xn(b):
                pool.wait_ge(xn_ready, b + 1)
                wait_free(pool, pv_done, T, b, 0)
                apart(pool)
                nc.gpsimd.tensor_copy(xn_hi[:, :, :], xn[:, :, :]).then_inc(xn_hi_ready, 1)

            def normalize_x1(b):
                wait_free(pool, x2T_turned, 1, b, 0)
                apart(pool)
                normalized(ln_x1, x1, x2n, x2n_ready)

            def shift_x1(b):
                pool.wait_ge(x1_tail_loaded, b * 16 + 16)
                wait_free(pool, y_ready, 1, b, 0)
                apart(pool)
                shifted(ln_y, x1_tail, ffn_base, ffn_base_ready)

            def scaled_eps(b):
                pool.wait_ge(exp_done, b * T + T)
                nc.gpsimd.tensor_tensor(rs_squared[:, :], row_sum[:, :], row_sum[:, :], ALU.mult).then_inc(rs_chain, 1)
                pool.wait_ge(rs_chain, b * 2 + 1)
                apart(pool)
                nc.gpsimd.tensor_scalar(rs_eps[:, :], rs_squared[:, :], EPS, 1.0, ALU.mult, ALU.mult).then_inc(rs_chain, 1)
                pool.wait_ge(rs_chain, b * 2 + 2)

            def shift_x(b):
                pool.wait_ge(x_res_loaded, b * 16 + 16)
                wait_free(pool, x1_ready, 1, b, 0)
                apart(pool)
                shifted(ln_att, x_res, att_base, att_base_ready)

            def step(st):
                a, b, g = st.att, st.mid, st.tail
                if a is not None:
                    high_xn(a)
                if st.prep is not None:
                    rstd(ln_x, st.prep)
                    normalize_x(st.prep)
                if g is not None:
                    rstd(ln_y, g)
                    shift_x1(g)
                if b is not None:
                    rstd(ln_x1, b)
                    normalize_x1(b)
                if a is not None:
                    scaled_eps(a)
                    rstd(ln_att, a, rs_eps[:, :])
                    shift_x(a)

            def start():
                rstd(ln_x, 0)
                normalize_x(0)
                high_xn(0)
                rstd(ln_x, 1)
                normalize_x(1)
                scaled_eps(0)
                high_xn(1)
                rstd(ln_att, 0, rs_eps[:, :])
                shift_x(0)
                rstd(ln_x, 2)
                normalize_x(2)
                rstd(ln_x1, 0)
                normalize_x1(0)
                scaled_eps(1)
                rstd(ln_att, 1, rs_eps[:, :])
                shift_x(1)

            def finish():
                rstd(ln_x1, N - 1)
                normalize_x1(N - 1)
                rstd(ln_y, N - 3)
                shift_x1(N - 3)
                rstd(ln_y, N - 2)
                shift_x1(N - 2)
                rstd(ln_y, N - 1)
                shift_x1(N - 1)

            nc.gpsimd.memset(ident[:, :], 0.0).then_inc(consts_zeroed, 1)
            nc.gpsimd.memset(minus_half[:, :], -0.5).then_inc(consts_zeroed, 1)
            nc.gpsimd.memset(ones[:, :], 1.0).then_inc(consts_ready, 1)
            pool.wait_ge(consts_zeroed, 2)
            nc.gpsimd.affine_select(out=ident[:, :], in_=ident[:, :], compare_op=ALU.not_equal, fill=1.0, base=0,
                                    pattern=[[-1, P]], channel_multiplier=1).then_inc(consts_ready, 1)
            start()
            steps(pool, step)
            finish()


def kernel(L0_attn_x, L0_attn_w_lhs, L0_attn_w_rhs, L0_ffn_w1_w, L0_ffn_w1_s, L0_ffn_w2_w, L0_ffn_w2_s,
           L0_ffn_h1_w, L0_ffn_h1_s, L0_ffn_h2_w, L0_ffn_h2_s, L0_ffn_w3_w, L0_ffn_w3_s):
    import numpy as np
    import concourse.bacc as bacc
    from concourse.bass_utils import run_bass_kernel_spmd

    def tiles(w):
        w = np.asarray(w)
        return w.T.reshape(-1, 128, w.shape[0]).transpose(1, 0, 2).reshape(128, -1)

    def column(s):
        return np.asarray(s).reshape(-1, 128).T

    arrays = {
        "x_dram": np.ascontiguousarray(L0_attn_x),
        "weights_dram": np.concatenate(
            [tiles(w) for w in (L0_ffn_w1_w, L0_ffn_w2_w, L0_ffn_w3_w, L0_ffn_h1_w, L0_ffn_h2_w)], axis=1),
        "columns_dram": np.concatenate(
            [column(s) for s in (L0_ffn_w1_s, L0_ffn_w2_s, L0_ffn_h1_s, L0_ffn_h2_s, L0_ffn_w3_s,
                                 L0_attn_w_lhs, L0_attn_w_rhs)], axis=1),
    }
    nc = bacc.Bacc("TRN2", target_bir_lowering=False, num_devices=1)
    args = [nc.dram_tensor(n, a.shape, mybir.dt.from_np(a.dtype), kind="ExternalInput").ap() for n, a in arrays.items()]
    shape = arrays["x_dram"].shape
    args.append(nc.dram_tensor("out_dram", shape, mybir.dt.float32, kind="ExternalOutput").ap())
    sandwich_kernel(nc, *args)
    r = run_bass_kernel_spmd(nc, [arrays], core_ids=[0])
    return r.results[0]["out_dram"]
```
